# Optimizing a Trainium2 kernel written in Bass

```python
import numpy as np
import jax
import jax.numpy as jnp

def _softmax(x, axis=-1):
    return jax.nn.softmax(x, axis=axis)

def _gelu(x):
    return jax.nn.gelu(x, approximate=True)

def _silu(x):
    return jax.nn.silu(x)

def _sigmoid(x):
    return jax.nn.sigmoid(x)

def _layernorm(x, axis=-1, eps=1e-05):
    m = jnp.mean(x, axis=axis, keepdims=True)
    v = jnp.var(x, axis=axis, keepdims=True)
    return (x - m) / jnp.sqrt(v + eps)

def _scatter_add(tgt, idx, src, axis=0):
    return tgt.at[idx].add(src)

def _segment_sum(src, seg, n):
    return jax.ops.segment_sum(src, seg, n)
kernel_name = 'mk_early_fusion_d1_tok_img1024_r4_94bd29'

def setup_inputs(seed: int=0):
    np.random.seed(seed)
    _w = jnp.asarray

    def _rec_inputs():
        import jax
        import jax.numpy as jnp
        _rk = jax.random.key(seed)
        x = -0.00016672 + 0.999947 * jax.random.normal(jax.random.fold_in(_rk, 1), (32, 3, 96, 96), jnp.float32)
        txt = -0.000312475 + 0.578156 * jax.random.normal(jax.random.fold_in(_rk, 2), (32, 32, 256), jnp.float32)
        return (x, txt)
    x, txt = _rec_inputs()

    def _L0_tok_setup():
        import jax, jax.numpy as jnp
        import numpy as np
        IMAGE_SIZE = 96
        PATCH = 16
        N_EMBD = 256
        C = 3
        N_PATCHES = (IMAGE_SIZE // PATCH) ** 2
        PATCH_DIM = C * PATCH * PATCH
        key = jax.random.key(seed)
        kx, kw, kb, kp = jax.random.split(key, 4)
        B = 64
        x = jax.random.normal(kx, (B, C, IMAGE_SIZE, IMAGE_SIZE), dtype=jnp.float32)
        bound = 1.0 / np.sqrt(PATCH_DIM)
        W = jax.random.uniform(kw, (N_EMBD, PATCH_DIM), minval=-bound, maxval=bound, dtype=jnp.float32)
        b = jax.random.uniform(kb, (N_EMBD,), minval=-bound, maxval=bound, dtype=jnp.float32)
        pos_embd = jax.random.normal(kp, (1, N_PATCHES, N_EMBD), dtype=jnp.float32) * 0.02
        return {'x': x, 'W': W, 'b': b, 'pos_embd': pos_embd}
    _L0_tok_all = _L0_tok_setup()
    _L0_tok_in = {k: v for k, v in _L0_tok_all.items() if k in ('W', 'b', 'pos_embd')}
    del _L0_tok_all

    def _L0_attn_setup():
        import jax, jax.numpy as jnp
        import numpy as np
        DIM = 256
        H = 16
        DH = DIM // H

        def _l2norm(a):
            n = jnp.linalg.norm(a, axis=-1, keepdims=True)
            return a / jnp.maximum(n, 1e-12)
        key = jax.random.key(seed)
        ks = jax.random.split(key, 6)
        B, T = (4, 1024)
        s = 0.02
        return {'x': jax.random.normal(ks[0], (B, T, DIM), jnp.float32), 'Wqkv': jax.random.normal(ks[1], (3 * DIM, DIM), jnp.float32) * s, 'Wg': jax.random.normal(ks[2], (H, DIM), jnp.float32) * s, 'bg': jnp.zeros((H,), jnp.float32), 'Wb': jax.random.normal(ks[3], (H, DIM), jnp.float32) * s, 'bb': jnp.zeros((H,), jnp.float32), 'Wout': jax.random.normal(ks[4], (DIM, DIM), jnp.float32) * s}
    _L0_attn_all = _L0_attn_setup()
    _L0_attn_in = {k: v for k, v in _L0_attn_all.items() if k in ('Wqkv', 'Wg', 'bg', 'Wb', 'bb', 'Wout')}
    del _L0_attn_all

    def _L0_ffn_setup():
        import jax, jax.numpy as jnp
        import numpy as np
        D = 256
        F = 256
        E = 8
        K = 2
        B, T = (2, 512)

        def _moe_forward(x, router_w, w1, w2, shared_gate_up, shared_down, shared_gate_w):
            b, t, d = x.shape
            xf = x.reshape(-1, d)
            n = xf.shape[0]
            logits = xf @ router_w
            probs = jax.nn.softmax(logits, axis=-1)
            topw, topi = jax.lax.top_k(probs, K)
            combine = jnp.zeros((n, E), dtype=probs.dtype).at[jnp.arange(n)[:, None], topi].add(topw)
            h = jax.nn.silu(jnp.einsum('nd,edf->nef', xf, w1))
            ye = jnp.einsum('nef,efd->ned', h, w2)
            routed = jnp.einsum('ne,ned->nd', combine, ye)
            gu = xf @ shared_gate_up
            gate, up = (gu[:, :F], gu[:, F:])
            shared = jax.nn.silu(gate) * up @ shared_down
            shared = jax.nn.sigmoid(xf @ shared_gate_w) * shared
            return (routed + shared).reshape(b, t, d)
        key = jax.random.key(seed)
        ks = jax.random.split(key, 7)
        std = 0.02
        x = jax.random.normal(ks[0], (B, T, D), dtype=jnp.float32)
        router_w = jax.random.normal(ks[1], (D, E), dtype=jnp.float32) * std
        w1 = jax.random.normal(ks[2], (E, D, F), dtype=jnp.float32) * std
        w2 = jax.random.normal(ks[3], (E, F, D), dtype=jnp.float32) * std
        shared_gate_up = jax.random.normal(ks[4], (D, 2 * F), dtype=jnp.float32) * std
        shared_down = jax.random.normal(ks[5], (F, D), dtype=jnp.float32) * std
        shared_gate_w = jax.random.normal(ks[6], (D, 1), dtype=jnp.float32) * std
        return {'x': x, 'router_w': router_w, 'w1': w1, 'w2': w2, 'shared_gate_up': shared_gate_up, 'shared_down': shared_down, 'shared_gate_w': shared_gate_w}
    _L0_ffn_all = _L0_ffn_setup()
    _L0_ffn_in = {k: v for k, v in _L0_ffn_all.items() if k in ('router_w', 'w1', 'w2', 'shared_gate_up', 'shared_down', 'shared_gate_w')}
    del _L0_ffn_all
    return {'x': x, 'txt': txt, 'L0_tok_W': _L0_tok_in['W'], 'L0_tok_b': _L0_tok_in['b'], 'L0_tok_pos_embd': _L0_tok_in['pos_embd'], 'L0_attn_Wqkv': _L0_attn_in['Wqkv'], 'L0_attn_Wg': _L0_attn_in['Wg'], 'L0_attn_bg': _L0_attn_in['bg'], 'L0_attn_Wb': _L0_attn_in['Wb'], 'L0_attn_bb': _L0_attn_in['bb'], 'L0_attn_Wout': _L0_attn_in['Wout'], 'L0_ffn_router_w': _L0_ffn_in['router_w'], 'L0_ffn_w1': _L0_ffn_in['w1'], 'L0_ffn_w2': _L0_ffn_in['w2'], 'L0_ffn_shared_gate_up': _L0_ffn_in['shared_gate_up'], 'L0_ffn_shared_down': _L0_ffn_in['shared_down'], 'L0_ffn_shared_gate_w': _L0_ffn_in['shared_gate_w']}

def reference(x, txt, L0_tok_W, L0_tok_b, L0_tok_pos_embd, L0_attn_Wqkv, L0_attn_Wg, L0_attn_bg, L0_attn_Wb, L0_attn_bb, L0_attn_Wout, L0_ffn_router_w, L0_ffn_w1, L0_ffn_w2, L0_ffn_shared_gate_up, L0_ffn_shared_down, L0_ffn_shared_gate_w):
    import jax
    import jax.numpy as jnp

    def _L0_tok_ref(x, W, b, pos_embd):
        import jax, jax.numpy as jnp
        import numpy as np
        IMAGE_SIZE = 96
        PATCH = 16
        N_EMBD = 256
        C = 3
        N_PATCHES = (IMAGE_SIZE // PATCH) ** 2
        PATCH_DIM = C * PATCH * PATCH
        B, Cc, H, Wd = x.shape
        p = PATCH
        Hp, Wp = (H // p, Wd // p)
        patches = x.reshape(B, Cc, Hp, p, Wp, p)
        patches = patches.transpose(0, 2, 4, 1, 3, 5)
        patches = patches.reshape(B, Hp * Wp, Cc * p * p)
        out = jnp.einsum('bnd,ed->bne', patches, W) + b + pos_embd
        return out

    def _L0_attn_ref(x, Wqkv, Wg, bg, Wb, bb, Wout):
        import jax, jax.numpy as jnp
        import numpy as np
        DIM = 256
        H = 16
        DH = DIM // H

        def _l2norm(a):
            n = jnp.linalg.norm(a, axis=-1, keepdims=True)
            return a / jnp.maximum(n, 1e-12)
        B, T, D = x.shape
        qkv = (x @ Wqkv.T).reshape(B, T, 3, H, DH)
        q = _l2norm(qkv[:, :, 0])
        k = _l2norm(qkv[:, :, 1])
        v = qkv[:, :, 2]
        alpha = jax.nn.sigmoid(x @ Wg.T + bg)
        beta = jax.nn.sigmoid(x @ Wb.T + bb)
        qT = jnp.moveaxis(q, 1, 0)
        kT = jnp.moveaxis(k, 1, 0)
        vT = jnp.moveaxis(v, 1, 0)
        aT = jnp.moveaxis(alpha, 1, 0)
        bT = jnp.moveaxis(beta, 1, 0)
        S0 = jnp.zeros((B, H, DH, DH), jnp.float32)

        def step(S, inp):
            q_t, k_t, v_t, a_t, b_t = inp
            Sk = jnp.einsum('bhij,bhj->bhi', S, k_t)
            a = a_t[..., None, None]
            b = b_t[..., None, None]
            S = a * (S - b * Sk[..., :, None] * k_t[..., None, :]) + b * v_t[..., :, None] * k_t[..., None, :]
            o = jnp.einsum('bhij,bhj->bhi', S, q_t)
            return (S, o)
        _, outs = jax.lax.scan(step, S0, (qT, kT, vT, aT, bT))
        out = jnp.moveaxis(outs, 0, 1).reshape(B, T, D)
        return out @ Wout.T

    def _L0_ffn_ref(x, router_w, w1, w2, shared_gate_up, shared_down, shared_gate_w):
        import jax, jax.numpy as jnp
        import numpy as np
        D = 256
        F = 256
        E = 8
        K = 2
        B, T = (2, 512)

        def _moe_forward(x, router_w, w1, w2, shared_gate_up, shared_down, shared_gate_w):
            b, t, d = x.shape
            xf = x.reshape(-1, d)
            n = xf.shape[0]
            logits = xf @ router_w
            probs = jax.nn.softmax(logits, axis=-1)
            topw, topi = jax.lax.top_k(probs, K)
            combine = jnp.zeros((n, E), dtype=probs.dtype).at[jnp.arange(n)[:, None], topi].add(topw)
            h = jax.nn.silu(jnp.einsum('nd,edf->nef', xf, w1))
            ye = jnp.einsum('nef,efd->ned', h, w2)
            routed = jnp.einsum('ne,ned->nd', combine, ye)
            gu = xf @ shared_gate_up
            gate, up = (gu[:, :F], gu[:, F:])
            shared = jax.nn.silu(gate) * up @ shared_down
            shared = jax.nn.sigmoid(xf @ shared_gate_w) * shared
            return (routed + shared).reshape(b, t, d)
        return _moe_forward(x, router_w, w1, w2, shared_gate_up, shared_down, shared_gate_w)
    h = _L0_tok_ref(x, L0_tok_W, L0_tok_b, L0_tok_pos_embd)
    h = jnp.concatenate([h, txt], axis=1)
    h = h + _L0_attn_ref(_layernorm(h, axis=-1), L0_attn_Wqkv, L0_attn_Wg, L0_attn_bg, L0_attn_Wb, L0_attn_bb, L0_attn_Wout)
    h = h + _L0_ffn_ref(_layernorm(h, axis=-1), L0_ffn_router_w, L0_ffn_w1, L0_ffn_w2, L0_ffn_shared_gate_up, L0_ffn_shared_down, L0_ffn_shared_gate_w)
    return h

_drawn_inputs = setup_inputs


def setup_inputs(seed=0):
    import zlib

    import numpy as np

    out = dict(_drawn_inputs(seed))
    spreads = {'L0_attn_bg': (0.0, 2.0), 'L0_attn_bb': (0.0, 2.0)}
    factors = {'L0_attn_Wg': 26.885,
     'L0_attn_Wb': 8.0,
     'L0_ffn_router_w': 2.824,
     'L0_ffn_shared_gate_up': 3.796,
     'L0_ffn_shared_down': 3.794,
     'L0_ffn_shared_gate_w': 8.0}
    for name, (base, spread) in spreads.items():
        noise = np.random.default_rng([zlib.crc32(name.encode()), seed]).standard_normal(out[name].shape)
        drawn = base * np.exp(spread * noise) if base else spread * noise
        out[name] = jnp.asarray(drawn.astype(out[name].dtype))
    for name, factor in factors.items():
        out[name] = (out[name] * factor).astype(out[name].dtype)
    return out
```

```python
from contextlib import ExitStack

import concourse.bass as bass
from concourse import mybir

F32 = mybir.dt.float32
U32 = mybir.dt.uint32
ALU = mybir.AluOpType
ACT = mybir.ActivationFunctionType
AX = mybir.AxisListType

P = 128
B = 32
D = 256
KD = D // P
H, DH = 16, 16
PATCHES, TXT = 36, 32
T = PATCHES + TXT
STEPS = P // B
TILES = T // STEPS
PATCH_TILES = PATCHES // STEPS
PD = 768
KP = PD // P
HG = 4
GH = H // HG
GW = GH * DH
GC = 3 * GW + 2 * GH
E = 8
F = 256
EPS_LN = 1e-5
EPS_N2 = 1e-24
BANK = 512
MOVES = 16 * STEPS * HG


def fused_block(nc, patches, txt, w_patch, patch_bias, w_qkvg, gate_bias, w_out, w_router, w_up, w_down,
                w_shared_up, w_shared_down, selector, identity, out):
    with ExitStack() as ctx:
        def sb(name, shape, dt=F32):
            return ctx.enter_context(nc.sbuf_tensor(name, shape, dt))

        def sem(name):
            return ctx.enter_context(nc.semaphore(name))

        wp = sb("wp", [P, KP, D])
        pbias = sb("pbias", [STEPS + 1, PATCH_TILES, D])
        sel = sb("sel", [STEPS + 1, P])
        wq = sb("wq", [P, KD, HG * GC])
        gbias = sb("gbias", [P, 2 * GH])
        wo = sb("wo", [P, KD, D])
        wr = sb("wr", [P, KD, E + 1])
        wu = sb("wu", [P, E, KD, F])
        wd = sb("wd", [P, E, KD, D])
        wsu = sb("wsu", [P, KD, 2 * F])
        wsd = sb("wsd", [P, KD, D])
        ident = sb("ident", [P, P])
        minus_half = sb("minus_half", [P, 2 * GH * STEPS])
        iota8 = sb("iota8", [P, E])

        xin = sb("xin", [P, 2, KP, P])
        h_all = sb("h_all", [P, TILES, D])
        xn = sb("xn", [P, D])
        xT = sb("xT", [P, KD, P])
        qkvg = sb("qkvg", [P, HG * GC])
        rin = sb("rin", [P, 2, STEPS, GC])
        sq = sb("sq", [P, STEPS, 2 * GW])
        n2 = sb("n2", [P, STEPS, 2, GH])
        n2c = sb("n2c", [P, STEPS, 2, GH])
        inv = sb("inv", [P, STEPS, 2, GH])
        gz = sb("gz", [P, STEPS, 2 * GH])
        gt = sb("gt", [P, STEPS, 2 * GH])
        gates = sb("gates", [P, 2, STEPS, 2, GH])
        ia = sb("ia", [P, 2, STEPS, 2, GH])
        iab = sb("iab", [P, STEPS, GH])
        vb = sb("vb", [P, 2, STEPS, GW])
        pq = sb("pq", [P, STEPS, GH, DH])
        kqr = sb("kqr", [P, STEPS, GH])
        kq = sb("kq", [P, 2, STEPS, GH])
        S = sb("S", [P, 2, GH, DH, DH])
        prod = sb("prod", [P, GH, DH, DH])
        rsum = sb("rsum", [P, GW])
        ub = sb("ub", [P, STEPS, GW])
        outer = sb("outer", [P, GH, DH, DH])
        qprod = sb("qprod", [P, GH * DH, DH])
        tree8 = sb("tree8", [P, GH * DH, 8])
        tree4 = sb("tree4", [P, GH * DH, 4])
        tree2 = sb("tree2", [P, GH * DH, 2])
        oq = sb("oq", [P, STEPS, GW])
        o1 = sb("o1", [P, STEPS, GW])
        o2 = sb("o2", [P, STEPS, GW])
        og = sb("og", [P, STEPS, GW])
        otok = sb("otok", [P, D])
        oT = sb("oT", [P, KD, P])
        h1 = sb("h1", [P, 2, D])
        x2n = sb("x2n", [P, D])
        x2T = sb("x2T", [P, 2, KD, P])
        stat = sb("stat", [P, 2, 6])
        mv = sb("mv", [P, 2, 2])
        veps = sb("veps", [P, 2, 1])
        rstd = sb("rstd", [P, 2, 1])
        carrier = sb("carrier", [P, 1])
        lg = sb("lg", [P, E + 1])
        top8 = sb("top8", [P, 8])
        topi = sb("topi", [P, 8], U32)
        topf = sb("topf", [P, 8])
        z9 = sb("z9", [P, E + 1])
        t9 = sb("t9", [P, E + 1])
        num = sb("num", [P, E])
        den = sb("den", [P, E])
        rden = sb("rden", [P, E])
        ex = sb("ex", [P, E])
        esum = sb("esum", [P, 1])
        rsm = sb("rsm", [P, 1])
        mask1 = sb("mask1", [P, E])
        mask2 = sb("mask2", [P, E])
        comb = sb("comb", [P, 2, E + 1])
        hs = sb("hs", [P, 4, 2, KD, P])
        sg = sb("sg", [P, KD, P])
        hsh = sb("hsh", [P, KD, P])
        acc = sb("acc", [P, 2, D])

        bank = [ctx.enter_context(nc.psum_tensor(f"bank{i}", [P, BANK], F32)) for i in range(4)]
        kk = ctx.enter_context(nc.psum_tensor("kk", [P, 2, 2, STEPS, GH, DH], F32))
        decayed = ctx.enter_context(nc.psum_tensor("decayed", [P, GH, DH, DH], F32))

        ld_patch, ld_attn, ld_txt, ld_router, ld_up, ld_down, ld_shared = (
            sem(n) for n in ("ld_patch", "ld_attn", "ld_txt", "ld_router", "ld_up", "ld_down", "ld_shared"))
        xin_in, rin_in, otok_in, acc_free = (
            [sem(f"{n}{k}") for k in range(2)] for n in ("xin_in", "rin_in", "otok_in", "acc_free"))
        const_ready = sem("const_ready")
        pe_h, pe_xT, pe_qkv, pe_oT, pe_wout, pe_x2T, pe_router, pe_up, pe_gu, pe_down = (
            sem(n) for n in ("pe_h", "pe_xT", "pe_qkv", "pe_oT", "pe_wout", "pe_x2T", "pe_router", "pe_up", "pe_gu",
                             "pe_down"))
        act_h, act_xT, act_qkv, act_oT, act_x2T, act_hs, act_sg, act_sq, act_gt, act_t9, act_decay = (
            sem(n) for n in ("act_h", "act_xT", "act_qkv", "act_oT", "act_x2T", "act_hs", "act_sg", "act_sq",
                             "act_gt", "act_t9", "act_decay"))
        pool_rstd1, pool_rstd2, pool_inv, pool_qprod, pool_tree, pool_oq = (
            sem(n) for n in ("pool_rstd1", "pool_rstd2", "pool_inv", "pool_qprod", "pool_tree", "pool_oq"))
        (dve_st1, dve_st2, dve_xn, dve_x2n, dve_h1, dve_gz, dve_n2, dve_n2c, dve_gates, dve_prep, dve_prod, dve_rsum,
         dve_u, dve_outer, dve_state, dve_o12, dve_o, dve_logits, dve_z9, dve_route, dve_comb, dve_acc,
         dve_gu, dve_gsum) = (
            sem(n) for n in ("dve_st1", "dve_st2", "dve_xn", "dve_x2n", "dve_h1", "dve_gz", "dve_n2", "dve_n2c",
                             "dve_gates", "dve_prep", "dve_prod", "dve_rsum", "dve_u", "dve_outer", "dve_state",
                             "dve_o12", "dve_o", "dve_logits", "dve_z9", "dve_route", "dve_comb", "dve_acc",
                             "dve_gu", "dve_gsum"))

        block = ctx.enter_context(nc.Block())

        def stages(i):
            return {"A": 0 <= i + 1 < TILES, "R": 0 <= i < TILES, "O": 1 <= i <= TILES, "M": 2 <= i <= TILES + 1,
                    "patch": 0 <= i + 1 < PATCH_TILES, "fetch": i + 2 < PATCH_TILES}

        FIRST, LAST = -1, TILES + 1

        def run(eng, body):
            def peeled(i):
                body(i, i % 2, stages(i), lambda off: (i + off) // 2)

            def pairs(first, last):
                with eng.Fori(0, (last - first) // 2) as pair:
                    for n in range(2):
                        c = first + n
                        body(pair * 2 + c, c % 2, stages(c), lambda off: pair + (c + off) // 2)

            for i in range(FIRST, 3):
                peeled(i)
            pairs(3, PATCH_TILES - 2)
            peeled(PATCH_TILES - 2)
            pairs(PATCH_TILES - 1, TILES - 1)
            for i in range(TILES - 1, LAST + 1):
                peeled(i)

        bank_order = [
            [("oT", "O", -1, act_oT, 1, 1), ("up1", "M", -2, act_hs, 4, 2), ("down1", "M", -2, dve_acc, 5, 2),
             ("down2", "M", -2, dve_acc, 5, 3), ("downS", "M", -2, dve_acc, 5, 5)],
            [("h", "patch", 1, act_h, 1, 1), ("down0", "M", -2, dve_acc, 5, 1), ("qkv0", "A", 1, act_qkv, 2, 1),
             ("gu", "M", -2, dve_gu, 1, 1), ("router", "O", -1, dve_logits, 1, 1)],
            [("up0", "M", -2, act_hs, 4, 1), ("xT", "A", 1, act_xT, 1, 1), ("qkv1", "A", 1, act_qkv, 2, 2),
             ("x2T", "O", -1, act_x2T, 1, 1)],
            [("wout", "O", -1, dve_h1, 1, 1), ("up2", "M", -2, act_hs, 4, 3), ("up3", "M", -2, act_hs, 4, 4),
             ("down3", "M", -2, dve_acc, 5, 4)],
        ]

        def take(pe, name, i, st, before):
            for b, order in enumerate(bank_order):
                names = [g[0] for g in order]
                if name in names:
                    at = names.index(name)
                    back = [(g, 0, st) for g in reversed(order[:at])] + [(g, -1, before) for g in reversed(order)]
                    for (_, stage, off, s, per, nth), turn, live in back:
                        if live[stage]:
                            pe.wait_ge(s, (i + (off + turn)) * per + nth)
                            break
                    return bank[b]

        @block.sync
        def _(sp):
            sp.dma_start(wp[:], w_patch).then_inc(ld_patch, 16)
            sp.dma_start(pbias[:], patch_bias).then_inc(ld_patch, 16)
            sp.dma_start(sel[:], selector).then_inc(ld_patch, 16)
            sp.dma_start(xin[:, 0], patches[0]).then_inc(xin_in[0], 16)
            sp.dma_start(ident[:], identity).then_inc(ld_attn, 16)
            sp.dma_start(wq[:], w_qkvg).then_inc(ld_attn, 16)
            sp.dma_start(gbias[:], gate_bias).then_inc(ld_attn, 16)
            sp.dma_start(wo[:], w_out).then_inc(ld_attn, 16)
            sp.dma_start(wr[:], w_router).then_inc(ld_router, 16)
            sp.dma_start(wu[:], w_up).then_inc(ld_up, 16)
            sp.dma_start(wd[:], w_down).then_inc(ld_down, 16)
            sp.dma_start(wsu[:], w_shared_up).then_inc(ld_shared, 16)
            sp.dma_start(wsd[:], w_shared_down).then_inc(ld_shared, 16)
            sp.dma_start(h_all[:, PATCH_TILES:TILES], txt).then_inc(ld_txt, 16)

            def body(i, par, st, half):
                if st["fetch"]:
                    if not isinstance(i, int) or i >= 0:
                        sp.wait_ge(pe_h, i + 1)
                    sp.dma_start(xin[:, par], patches[i + 2]).then_inc(xin_in[par], 16)
                if st["A"]:
                    sp.wait_ge(act_qkv, (i + 2) * 2)
                    for s in range(STEPS):
                        for g in range(HG):
                            sp.dma_start(rin[g * B:(g + 1) * B, 1 - par, s, :],
                                         qkvg[s * B:(s + 1) * B, g * GC:(g + 1) * GC]).then_inc(rin_in[1 - par], 16)
                if st["R"]:
                    sp.wait_ge(dve_o, i + 1)
                    for s in range(STEPS):
                        for g in range(HG):
                            sp.dma_start(otok[s * B:(s + 1) * B, g * GW:(g + 1) * GW],
                                         og[g * B:(g + 1) * B, s, :]).then_inc(otok_in[par], 16)
                if st["M"]:
                    sp.wait_ge(dve_acc, (i - 1) * 5)
                    sp.dma_start(out[i - 2], acc[:, par]).then_inc(acc_free[par], 16)

            run(sp, body)
            for k in range(2):
                sp.wait_ge(acc_free[k], 16 + 16 * ((TILES + 1 - k) // 2))

        @block.tensor
        def _(pe):
            def matmuls(dst, pairs, done=None):
                for n, (l, r) in enumerate(pairs):
                    mm = pe.matmul(dst, l, r, start=(n == 0), stop=(n == len(pairs) - 1))
                if done is not None:
                    mm.then_inc(done, 1)

            def body(i, par, st, half):
                before = stages(i - 1) if isinstance(i, int) else st
                first = isinstance(i, int) and i == FIRST

                def up(k):
                    dst = take(pe, f"up{k}", i, st, before)
                    if isinstance(i, int) and i == 2:
                        pe.wait_ge(ld_up, 16)
                    for e in range(2):
                        for f in range(KD):
                            c = (e * KD + f) * P
                            matmuls(dst[:, c:c + P],
                                    [(wu[:, 2 * k + e, d, f * P:(f + 1) * P], x2T[:, par, d, :]) for d in range(KD)],
                                    pe_up if (e, f) == (1, KD - 1) else None)

                def down(k):
                    dst = take(pe, f"down{k}", i, st, before)
                    if isinstance(i, int) and i == 2:
                        pe.wait_ge(ld_down, 16)
                    pe.wait_ge(act_hs, (i - 2) * 4 + k + 1)
                    for e in range(2):
                        matmuls(dst[:, e * D:(e + 1) * D],
                                [(hs[:, k, e, f, :], wd[:, 2 * k + e, f, :]) for f in range(KD)],
                                pe_down if e else None)

                if st["O"]:
                    dst = take(pe, "oT", i, st, before)
                    pe.wait_ge(otok_in[1 - par], (half(-1) + 1) * MOVES)
                    for d in range(KD):
                        tr = pe.transpose(dst[:, d * P:(d + 1) * P], otok[:, d * P:(d + 1) * P], ident[:])
                    tr.then_inc(pe_oT, 1)
                if st["patch"]:
                    dst = take(pe, "h", i, st, before)
                    if first:
                        pe.wait_ge(ld_patch, 48)
                    pe.wait_ge(xin_in[1 - par], (half(1) + 1) * 16)
                    mm = pe.matmul(dst[:, 0:D], sel[:], pbias[:, i + 1, :], start=True, stop=False)
                    for d in range(KP):
                        mm = pe.matmul(dst[:, 0:D], xin[:, 1 - par, d, :], wp[:, d, :], start=False, stop=(d == KP - 1))
                    mm.then_inc(pe_h, 1)
                if st["M"]:
                    pe.wait_ge(act_x2T, i - 1)
                    up(0)
                if st["O"]:
                    dst = take(pe, "wout", i, st, before)
                    pe.wait_ge(act_oT, i)
                    matmuls(dst[:, 0:D], [(oT[:, d, :], wo[:, d, :]) for d in range(KD)], pe_wout)
                if st["M"]:
                    up(1)
                    down(0)
                if st["A"]:
                    dst = take(pe, "xT", i, st, before)
                    if first:
                        pe.wait_ge(ld_attn, 64)
                    pe.wait_ge(dve_xn, i + 2)
                    for d in range(KD):
                        tr = pe.transpose(dst[:, d * P:(d + 1) * P], xn[:, d * P:(d + 1) * P], ident[:])
                    tr.then_inc(pe_xT, 1)
                if st["M"]:
                    up(2)
                    down(1)
                if st["A"]:
                    pe.wait_ge(act_xT, i + 2)
                    cols = HG * GC // 2
                    for n in range(2):
                        dst = take(pe, f"qkv{n}", i, st, before)
                        matmuls(dst[:, 0:cols], [(xT[:, d, :], wq[:, d, n * cols:(n + 1) * cols]) for d in range(KD)],
                                pe_qkv)
                if st["M"]:
                    up(3)
                    down(2)
                    dst = take(pe, "gu", i, st, before)
                    if isinstance(i, int) and i == 2:
                        pe.wait_ge(ld_shared, 32)
                    for f in range(2 * KD):
                        matmuls(dst[:, f * P:(f + 1) * P],
                                [(wsu[:, d, f * P:(f + 1) * P], x2T[:, par, d, :]) for d in range(KD)],
                                pe_gu if f == 2 * KD - 1 else None)
                if st["O"]:
                    dst = take(pe, "x2T", i, st, before)
                    pe.wait_ge(dve_x2n, i)
                    for d in range(KD):
                        tr = pe.transpose(dst[:, d * P:(d + 1) * P], x2n[:, d * P:(d + 1) * P], ident[:])
                    tr.then_inc(pe_x2T, 1)
                if st["M"]:
                    down(3)
                    dst = take(pe, "downS", i, st, before)
                    pe.wait_ge(dve_gu, i - 1)
                    matmuls(dst[:, 0:D], [(hsh[:, f, :], wsd[:, f, :]) for f in range(KD)], pe_down)
                if st["O"]:
                    dst = take(pe, "router", i, st, before)
                    if isinstance(i, int) and i == 1:
                        pe.wait_ge(ld_router, 16)
                    pe.wait_ge(act_x2T, i)
                    matmuls(dst[:, 0:E + 1], [(x2T[:, 1 - par, d, :], wr[:, d, :]) for d in range(KD)], pe_router)

            run(pe, body)

        @block.scalar
        def _(act):
            act.preload_act_table_set("silu_and_others")

            def body(i, par, st, half):
                def decay(s):
                    act.wait_ge(dve_state, i * STEPS + s + 1)
                    if s == 0:
                        act.wait_ge(dve_gates, i + 1)
                    for g in range(GH):
                        act.activation(decayed[:, g], S[:, (s + 1) % 2, g], ACT.Copy,
                                       scale=gates[:, par, s, 0, g:g + 1]).then_inc(act_decay, 1)

                def hidden(k):
                    act.wait_ge(pe_up, (i - 2) * 4 + k + 1)
                    if not isinstance(i, int) or i >= 3:
                        act.wait_ge(pe_down, (i - 3) * 5 + k + 1)
                    act.activation(hs[:, k].rearrange("p e f t -> p (e f t)"), bank[(2, 0, 3, 3)[k]][:], ACT.Silu)\
                       .then_inc(act_hs, 1)

                if st["R"]:
                    decay(0)
                if st["O"]:
                    act.wait_ge(pe_oT, i)
                    act.activation(oT[:].rearrange("p d t -> p (d t)"), bank[0][:, 0:D], ACT.Copy).then_inc(act_oT, 1)
                if st["patch"]:
                    act.wait_ge(pe_h, i + 2)
                    act.activation(h_all[:, i + 1, :], bank[1][:, 0:D], ACT.Copy).then_inc(act_h, 1)
                if st["M"]:
                    hidden(0)
                    hidden(1)
                if st["R"]:
                    decay(1)
                if st["A"]:
                    act.wait_ge(pe_xT, i + 2)
                    act.activation(xT[:].rearrange("p d t -> p (d t)"), bank[2][:, 0:D], ACT.Copy).then_inc(act_xT, 1)
                if st["M"]:
                    hidden(2)
                if st["A"]:
                    cols = HG * GC // 2
                    for n in range(2):
                        act.wait_ge(pe_qkv, (i + 1) * 2 + n + 1)
                        if not isinstance(i, int) or i >= 0:
                            act.wait_ge(rin_in[par], (half(0) + 1) * MOVES)
                        act.activation(qkvg[:, n * cols:(n + 1) * cols], bank[1 + n][:, 0:cols], ACT.Copy)\
                           .then_inc(act_qkv, 1)
                if st["R"]:
                    decay(2)
                if st["M"]:
                    hidden(3)
                if st["M"]:
                    act.wait_ge(pe_gu, i - 1)
                    if not isinstance(i, int) or i >= 3:
                        act.wait_ge(dve_gu, i - 2)
                    act.activation(sg[:].rearrange("p f t -> p (f t)"), bank[1][:, 0:F], ACT.Silu).then_inc(act_sg, 1)
                if st["A"]:
                    act.wait_ge(rin_in[1 - par], (half(1) + 1) * MOVES)
                    if not isinstance(i, int) or i >= 0:
                        act.wait_ge(dve_n2, i + 1)
                    act.activation(sq[:], rin[:, 1 - par, :, 0:2 * GW], ACT.Square).then_inc(act_sq, 1)
                    act.wait_ge(dve_gz, i + 2)
                    act.activation(gt[:], gz[:], ACT.Tanh, scale=0.5).then_inc(act_gt, 1)
                if st["R"]:
                    decay(3)
                if st["O"]:
                    act.wait_ge(pe_x2T, i)
                    act.activation(x2T[:, 1 - par].rearrange("p d t -> p (d t)"), bank[2][:, 0:D], ACT.Copy)\
                       .then_inc(act_x2T, 1)
                    act.wait_ge(dve_z9, i * 2)
                    act.activation(t9[:], z9[:], ACT.Tanh, scale=0.5).then_inc(act_t9, 1)

            run(act, body)

        @block.gpsimd
        def _(pool):
            pool.memset(minus_half[:], -0.5).then_inc(const_ready, 1)
            pool.iota(topi[:], pattern=[[1, 8]], base=0, channel_multiplier=0).then_inc(const_ready, 1)
            pool.wait_ge(const_ready, 2)
            pool.tensor_copy(iota8[:], topi[:]).then_inc(const_ready, 1)
            pool.wait_ge(const_ready, 3)

            def body(i, par, st, half):
                def read_out(s):
                    pool.wait_ge(dve_state, i * STEPS + s + 1)
                    q = rin[:, par, s, 0:GW].rearrange("p (h d) -> p h d", h=GH)
                    for g in range(GH):
                        ins = pool.tensor_tensor(qprod[:, g * DH:(g + 1) * DH, :], S[:, (s + 1) % 2, g],
                                                 q[:, g, :].unsqueeze(1).to_broadcast([P, DH, DH]), ALU.mult)
                    ins.then_inc(pool_qprod, 1)
                    at = i * STEPS + s
                    pool.wait_ge(pool_qprod, at + 1)
                    pool.tensor_tensor(tree8[:], qprod[:, :, 0:8], qprod[:, :, 8:16], ALU.add).then_inc(pool_tree, 1)
                    pool.wait_ge(pool_tree, at * 3 + 1)
                    pool.tensor_tensor(tree4[:], tree8[:, :, 0:4], tree8[:, :, 4:8], ALU.add).then_inc(pool_tree, 1)
                    pool.wait_ge(pool_tree, at * 3 + 2)
                    pool.tensor_tensor(tree2[:], tree4[:, :, 0:2], tree4[:, :, 2:4], ALU.add).then_inc(pool_tree, 1)
                    pool.wait_ge(pool_tree, at * 3 + 3)
                    if s == 0 and (not isinstance(i, int) or i >= 1):
                        pool.wait_ge(dve_o12, i * 2)
                    pool.tensor_tensor(oq[:, s, :], tree2[:, :, 0], tree2[:, :, 1], ALU.add).then_inc(pool_oq, 1)

                if st["R"]:
                    read_out(0)
                if st["O"]:
                    pool.wait_ge(dve_st2, i * 3)
                    pool.tensor_tensor(rstd[:, 1], veps[:, 1], minus_half[:, 0:1], ALU.pow).then_inc(pool_rstd2, 1)
                if st["A"]:
                    pool.wait_ge(dve_st1, (i + 2) * 3)
                    pool.tensor_tensor(rstd[:, 0], veps[:, 0], minus_half[:, 0:1], ALU.pow).then_inc(pool_rstd1, 1)
                if st["R"]:
                    read_out(1)
                    read_out(2)
                if st["A"]:
                    pool.wait_ge(dve_n2c, i + 2)
                    pool.tensor_tensor(inv[:].rearrange("p s k h -> p (s k h)"),
                                       n2c[:].rearrange("p s k h -> p (s k h)"), minus_half[:],
                                       ALU.pow).then_inc(pool_inv, 1)
                if st["R"]:
                    read_out(3)

            run(pool, body)

        @block.vector
        def _(dve):
            PREP, ROUTE = 9, 12
            dve.memset(S[:, 1], 0.0).then_inc(dve_state, 1)
            for k in range(2):
                dve.memset(acc[:, k], 0.0).then_inc(acc_free[k], 16)
            dve.wait_ge(const_ready, 3)

            def body(i, par, st, half):
                inner = not isinstance(i, int)

                def statistics(which, src, s, tile):
                    dve.bn_stats(stat[:, which], src).then_inc(s, 1)
                    dve.wait_ge(s, tile * 3 + 1)
                    dve.memset(carrier[:], 0.0)
                    dve.bn_aggr(mv[:, which], stat[:, which]).then_inc(s, 1)
                    dve.wait_ge(s, tile * 3 + 2)
                    dve.tensor_scalar(veps[:, which], mv[:, which, 1:2], EPS_LN, None, ALU.add).then_inc(s, 1)

                def residual():
                    dve.wait_ge(pe_wout, i)
                    dve.tensor_tensor(h1[:, 1 - par], bank[3][:, 0:D], h_all[:, i - 1, :], ALU.add)\
                       .then_inc(dve_h1, 1)
                    dve.wait_ge(dve_h1, i)
                    statistics(1, h1[:, 1 - par], dve_st2, i - 1)

                def norm_1_statistics():
                    if st["patch"]:
                        dve.wait_ge(act_h, i + 2)
                    else:
                        dve.wait_ge(ld_txt, 16)
                    statistics(0, h_all[:, i + 1, :], dve_st1, i + 1)

                def norm_2():
                    dve.wait_ge(pool_rstd2, i)
                    if inner or i >= 2:
                        dve.wait_ge(pe_x2T, i - 1)
                    dve.tensor_scalar(x2n[:], h1[:, 1 - par], mv[:, 1, 0:1], rstd[:, 1], ALU.subtract, ALU.mult)\
                       .then_inc(dve_x2n, 1)

                def norm_1():
                    dve.wait_ge(pool_rstd1, i + 2)
                    if inner or i >= 0:
                        dve.wait_ge(pe_xT, i + 1)
                    dve.tensor_scalar(xn[:], h_all[:, i + 1, :], mv[:, 0, 0:1], rstd[:, 0], ALU.subtract, ALU.mult)\
                       .then_inc(dve_xn, 1)

                down_bank = (1, 0, 0, 3, 0)

                def add_experts(k):
                    dve.wait_ge(pe_down, (i - 2) * 5 + k + 1)
                    if k == 0:
                        dve.wait_ge(acc_free[par], (half(-2) + 1) * 16)
                    for e in ([0, 1] if k < 4 else [0]):
                        src = h1[:, par] if (k, e) == (0, 0) else acc[:, par]
                        n = 2 * k + e
                        if (k, e) != (0, 0):
                            if e == 1:
                                dve.wait_ge(dve_gsum, (i - 2) * 4 + k + 1)
                            else:
                                dve.wait_ge(dve_acc, (i - 2) * 5 + k)
                        ins = dve.scalar_tensor_tensor(acc[:, par], bank[down_bank[k]][:, e * D:(e + 1) * D],
                                                       comb[:, par, n:n + 1], src, ALU.mult, ALU.add)
                        ins.then_inc(dve_gsum if (e == 0 and k < 4) else dve_acc, 1)

                def gated_up():
                    dve.wait_ge(act_sg, i - 1)
                    if inner or i >= 3:
                        dve.wait_ge(pe_down, (i - 2) * 5)
                    dve.tensor_tensor(hsh[:].rearrange("p f t -> p (f t)"), bank[1][:, F:2 * F],
                                      sg[:].rearrange("p f t -> p (f t)"), ALU.mult).then_inc(dve_gu, 1)

                def gate_inputs():
                    dve.wait_ge(rin_in[1 - par], (half(1) + 1) * MOVES)
                    if not inner and i == FIRST:
                        dve.wait_ge(ld_attn, 64)
                    dve.tensor_tensor(gz[:], rin[:, 1 - par, :, 3 * GW:GC],
                                      gbias[:].unsqueeze(1).to_broadcast([P, STEPS, 2 * GH]), ALU.add)\
                       .then_inc(dve_gz, 1)

                def norms():
                    dve.wait_ge(act_sq, i + 2)
                    dve.tensor_reduce(n2[:].rearrange("p s k h -> p s (k h)"),
                                      sq[:].rearrange("p s (m d) -> p s m d", d=DH), AX.X, ALU.add).then_inc(dve_n2, 1)
                    dve.wait_ge(dve_n2, i + 2)
                    dve.tensor_scalar(n2c[:], n2[:], EPS_N2, None, ALU.max).then_inc(dve_n2c, 1)

                def gate_values():
                    dve.wait_ge(act_gt, i + 2)
                    dve.tensor_scalar(gates[:, 1 - par].rearrange("p s k h -> p s (k h)"), gt[:], 0.5, 0.5, ALU.mult,
                                      ALU.add).then_inc(dve_gates, 1)

                def heads(ap):
                    return ap.rearrange("p s (h d) -> p s h d", h=GH)

                def over_width(ap):
                    return ap.unsqueeze(3).to_broadcast([P, STEPS, GH, DH])


                def prepare():
                    at = (i + 1) * PREP
                    q, k, v = (heads(rin[:, 1 - par, :, n * GW:(n + 1) * GW]) for n in range(3))
                    dve.wait_ge(pool_inv, i + 2)
                    dve.wait_ge(dve_gates, i + 2)
                    for n in range(2):
                        dve.tensor_tensor(ia[:, 1 - par, :, n, :], inv[:, :, n, :], gates[:, 1 - par, :, 0, :],
                                          ALU.mult).then_inc(dve_prep, 1)
                    dve.tensor_tensor(kk[:, 1 - par, 0], k, over_width(inv[:, :, 1, :]), ALU.mult).then_inc(dve_prep, 1)
                    dve.wait_ge(dve_prep, at + 2)
                    dve.tensor_tensor(iab[:], ia[:, 1 - par, :, 1, :], gates[:, 1 - par, :, 1, :], ALU.mult)\
                       .then_inc(dve_prep, 1)
                    dve.tensor_tensor(heads(vb[:, 1 - par]), v, over_width(gates[:, 1 - par, :, 1, :]), ALU.mult)\
                       .then_inc(dve_prep, 1)
                    dve.wait_ge(dve_prep, at + 4)
                    dve.tensor_tensor(kk[:, 1 - par, 1], k, over_width(iab[:]), ALU.mult).then_inc(dve_prep, 1)
                    dve.tensor_tensor(pq[:], kk[:, 1 - par, 0], q, ALU.mult).then_inc(dve_prep, 1)
                    dve.wait_ge(dve_prep, at + 7)
                    dve.tensor_reduce(kqr[:], pq[:], AX.X, ALU.add).then_inc(dve_prep, 1)
                    dve.wait_ge(dve_prep, at + 8)
                    dve.tensor_tensor(kq[:, 1 - par], kqr[:], inv[:, :, 0, :], ALU.mult).then_inc(dve_prep, 1)

                def step(s, fill):
                    t = i * STEPS + s
                    old, new = S[:, (s + 1) % 2], S[:, s % 2]
                    shape = [P, GH, DH, DH]
                    dve.wait_ge(dve_state, t + 1)
                    if s == 0:
                        dve.wait_ge(dve_prep, (i + 1) * PREP)
                    for g in range(GH):
                        ins = dve.tensor_tensor(prod[:, g], old[:, g],
                                                kk[:, par, 1, s, g].unsqueeze(1).to_broadcast([P, DH, DH]), ALU.mult)
                    ins.then_inc(dve_prod, 1)
                    fill()
                    dve.wait_ge(dve_prod, t + 1)
                    dve.tensor_reduce(rsum[:].rearrange("p (h r) -> p h r", h=GH), prod[:], AX.X, ALU.add)\
                       .then_inc(dve_rsum, 1)
                    fill()
                    dve.wait_ge(dve_rsum, t + 1)
                    dve.tensor_tensor(ub[:, s, :], vb[:, par, s, :], rsum[:], ALU.subtract).then_inc(dve_u, 1)
                    dve.wait_ge(dve_u, t + 1)
                    u = ub[:, s, :].rearrange("p (h r) -> p h r", h=GH)
                    for g in range(GH):
                        ins = dve.tensor_tensor(outer[:, g], u[:, g].unsqueeze(2).to_broadcast([P, DH, DH]),
                                                kk[:, par, 0, s, g].unsqueeze(1).to_broadcast([P, DH, DH]), ALU.mult)
                    ins.then_inc(dve_outer, 1)
                    fill()
                    dve.wait_ge(dve_outer, t + 1)
                    dve.wait_ge(act_decay, (t + 1) * GH)
                    if inner or i >= 1 or s >= 1:
                        dve.wait_ge(pool_qprod, t)
                    dve.tensor_tensor(new, decayed[:], outer[:], ALU.add).then_inc(dve_state, 1)
                    fill()

                def head_outputs():
                    dve.wait_ge(pool_oq, (i + 1) * STEPS)
                    dve.tensor_tensor(heads(o1[:]), heads(oq[:]), over_width(ia[:, par, :, 0, :]), ALU.mult)\
                       .then_inc(dve_o12, 1)
                    dve.tensor_tensor(heads(o2[:]), heads(ub[:]), over_width(kq[:, par]), ALU.mult).then_inc(dve_o12, 1)
                    dve.wait_ge(dve_o12, (i + 1) * 2)
                    if inner or i >= 1:
                        dve.wait_ge(otok_in[1 - par], (half(-1) + 1) * MOVES)
                    dve.tensor_tensor(og[:], o1[:], o2[:], ALU.add).then_inc(dve_o, 1)

                def route_inputs():
                    dve.wait_ge(pe_router, i)
                    dve.tensor_copy(lg[:], bank[1][:, 0:E + 1]).then_inc(dve_logits, 1)
                    dve.wait_ge(dve_logits, i)
                    dve.tensor_copy(z9[:, E:E + 1], lg[:, E:E + 1]).then_inc(dve_z9, 1)
                    dve.max(top8[:], lg[:, 0:E]).then_inc(dve_route, 1)
                    at = (i - 1) * ROUTE
                    dve.wait_ge(dve_route, at + 1)
                    dve.tensor_scalar(z9[:, 0:E], lg[:, 0:E], top8[:, 0:1], None, ALU.subtract).then_inc(dve_z9, 1)
                    dve.max_index(topi[:], top8[:], lg[:, 0:E]).then_inc(dve_route, 1)
                    dve.wait_ge(dve_route, at + 2)
                    dve.tensor_copy(topf[:], topi[:]).then_inc(dve_route, 1)
                    dve.wait_ge(dve_route, at + 3)
                    dve.tensor_scalar(mask1[:], iota8[:], topf[:, 0:1], None, ALU.is_equal).then_inc(dve_route, 1)
                    dve.wait_ge(dve_route, at + 4)
                    dve.scalar_tensor_tensor(mask2[:], iota8[:], topf[:, 1:2], mask1[:], ALU.is_equal, ALU.add)\
                       .then_inc(dve_route, 1)

                def route_weights():
                    at = (i - 1) * ROUTE
                    dve.wait_ge(act_t9, i)
                    dve.tensor_scalar(den[:], t9[:, 0:E], -1.0, 1.0, ALU.mult, ALU.add).then_inc(dve_route, 1)
                    dve.tensor_scalar(num[:], t9[:, 0:E], 1.0, None, ALU.add).then_inc(dve_route, 1)
                    dve.tensor_scalar(comb[:, 1 - par, E:E + 1], t9[:, E:E + 1], 0.5, 0.5, ALU.mult, ALU.add)\
                       .then_inc(dve_route, 1)
                    dve.wait_ge(dve_route, at + 8)
                    dve.reciprocal(rden[:], den[:]).then_inc(dve_route, 1)
                    dve.wait_ge(dve_route, at + 9)
                    dve.tensor_tensor(ex[:], num[:], rden[:], ALU.mult).then_inc(dve_route, 1)
                    dve.wait_ge(dve_route, at + 10)
                    dve.tensor_reduce(esum[:], ex[:], AX.X, ALU.add).then_inc(dve_route, 1)
                    dve.wait_ge(dve_route, at + 11)
                    dve.reciprocal(rsm[:], esum[:]).then_inc(dve_route, 1)
                    dve.wait_ge(dve_route, at + 12)
                    dve.scalar_tensor_tensor(comb[:, 1 - par, 0:E], ex[:], rsm[:], mask2[:], ALU.mult, ALU.mult)\
                       .then_inc(dve_comb, 1)

                fills = {(s, n): [] for s in range(STEPS) for n in range(4)}
                if st["O"]:
                    fills[0, 1] += [residual]
                if st["A"]:
                    fills[0, 2] += [norm_1_statistics]
                if st["M"]:
                    fills[0, 3] += [lambda: dve.wait_ge(dve_comb, i - 1), lambda: add_experts(0)]
                if st["A"]:
                    fills[1, 0] += [norm_1]
                if st["O"]:
                    fills[1, 1] += [norm_2]
                if st["M"]:
                    fills[1, 2] += [lambda: add_experts(1)]
                    fills[2, 1] += [lambda: add_experts(2)]
                    fills[2, 2] += [gated_up]
                    fills[2, 3] += [lambda: add_experts(3)]
                    fills[3, 0] += [lambda: add_experts(4)]
                if st["A"]:
                    fills[2, 3] += [gate_inputs]
                    fills[3, 1] += [norms]
                    fills[3, 2] += [gate_values]
                if st["O"]:
                    fills[3, 0] += [route_inputs]
                    fills[3, 3] += [route_weights]
                for s in range(STEPS):
                    if st["R"]:
                        turn = iter(range(4))

                        def fill(s=s, turn=turn):
                            for part in fills[s, next(turn)]:
                                part()
                        step(s, fill)
                    else:
                        for n in range(4):
                            for part in fills[s, n]:
                                part()
                if st["A"]:
                    prepare()
                if st["R"]:
                    head_outputs()

            run(dve, body)


def kernel(x, txt, L0_tok_W, L0_tok_b, L0_tok_pos_embd, L0_attn_Wqkv, L0_attn_Wg, L0_attn_bg, L0_attn_Wb, L0_attn_bb,
           L0_attn_Wout, L0_ffn_router_w, L0_ffn_w1, L0_ffn_w2, L0_ffn_shared_gate_up, L0_ffn_shared_down,
           L0_ffn_shared_gate_w):
    import numpy as np
    import concourse.bacc as bacc
    from concourse.bass_utils import run_bass_kernel_spmd

    def a(v):
        return np.asarray(v)

    def blocked(w):
        return a(w).reshape(-1, P, w.shape[-1]).transpose(1, 0, 2)

    side = int(PATCHES ** 0.5)
    px = x.shape[-1] // side
    patches = a(x).reshape(B, 3, side, px, side, px).transpose(2, 4, 1, 3, 5, 0)
    patches = patches.reshape(PATCH_TILES, STEPS, KP, P, B).transpose(0, 3, 2, 1, 4)
    text = a(txt).transpose(1, 0, 2).reshape(TILES - PATCH_TILES, P, D).transpose(1, 0, 2)
    pos = a(L0_tok_pos_embd).reshape(PATCH_TILES, STEPS, D).transpose(1, 0, 2)
    bias = np.broadcast_to(a(L0_tok_b), (1, PATCH_TILES, D))
    qkv = a(L0_attn_Wqkv).reshape(3, HG, GW, D)
    gates = np.stack([a(L0_attn_Wg), a(L0_attn_Wb)]).reshape(2, HG, GH, D)
    w_qkvg = np.concatenate([np.concatenate([*qkv[:, g], *gates[:, g]]) for g in range(HG)]).T
    gate_bias = np.concatenate([a(L0_attn_bg).reshape(HG, GH), a(L0_attn_bb).reshape(HG, GH)], axis=1)
    selector = np.concatenate([np.repeat(np.eye(STEPS), B, axis=1), np.ones((1, P))]).astype(np.float32)
    ins = {
        "patches": patches.reshape(PATCH_TILES, P, KP, P),
        "txt": text,
        "w_patch": blocked(a(L0_tok_W).T),
        "patch_bias": np.concatenate([pos, bias]),
        "w_qkvg": blocked(w_qkvg),
        "gate_bias": np.repeat(gate_bias, B, axis=0),
        "w_out": blocked(a(L0_attn_Wout).T),
        "w_router": blocked(np.concatenate([a(L0_ffn_router_w), a(L0_ffn_shared_gate_w)], axis=1)),
        "w_up": a(L0_ffn_w1).reshape(E, KD, P, F).transpose(2, 0, 1, 3),
        "w_down": a(L0_ffn_w2).reshape(E, KD, P, D).transpose(2, 0, 1, 3),
        "w_shared_up": blocked(L0_ffn_shared_gate_up),
        "w_shared_down": blocked(L0_ffn_shared_down),
        "selector": selector,
        "identity": np.eye(P, dtype=np.float32),
    }
    ins = {k: np.ascontiguousarray(v) for k, v in ins.items()}
    nc = bacc.Bacc("TRN2", target_bir_lowering=False, num_devices=1)
    aps = {k: nc.dram_tensor(k, v.shape, F32, kind="ExternalInput").ap() for k, v in ins.items()}
    out = nc.dram_tensor("out", (TILES, P, D), F32, kind="ExternalOutput").ap()
    fused_block(nc, out=out, **aps)
    got = run_bass_kernel_spmd(nc, [ins], core_ids=[0]).results[0]["out"]
    return got.reshape(T, B, D).transpose(1, 0, 2)
```

```python
from contextlib import ExitStack

import concourse.bass as bass
from concourse import mybir

F32 = mybir.dt.float32
U32 = mybir.dt.uint32
ALU = mybir.AluOpType
ACT = mybir.ActivationFunctionType
AX = mybir.AxisListType

P = 128
B = 32
D = 256
KD = D // P
H, DH = 16, 16
PATCHES, TXT = 36, 32
T = PATCHES + TXT
STEPS = P // B
TILES = T // STEPS
PATCH_TILES = PATCHES // STEPS
PD = 768
KP = PD // P
HG = 4
GH = H // HG
GW = GH * DH
GC = 3 * GW + 2 * GH
E = 8
F = 256
EPS_LN = 1e-5
EPS_N2 = 1e-24
BANK = 512
MOVES = 16 * 4
assert STEPS == HG == 4


def fused_block(nc, patches, txt, w_patch, patch_bias, w_qkvg, gate_bias, w_out, w_router, w_up, w_down,
                w_shared_up, w_shared_down, selector, identity, out):
    with ExitStack() as ctx:
        def sb(name, shape, dt=F32):
            return ctx.enter_context(nc.sbuf_tensor(name, shape, dt))

        def sem(name):
            return ctx.enter_context(nc.semaphore(name))

        wp = sb("wp", [P, KP, D])
        pbias = sb("pbias", [STEPS + 1, PATCH_TILES, D])
        sel = sb("sel", [STEPS + 1, P])
        wq = sb("wq", [P, KD, HG * GC])
        gbias = sb("gbias", [P, 2 * GH])
        wo = sb("wo", [P, KD, D])
        wr = sb("wr", [P, KD, E + 1])
        wu = sb("wu", [P, E, KD, F])
        wd = sb("wd", [P, E, KD, D])
        wsu = sb("wsu", [P, KD, 2 * F])
        wsd = sb("wsd", [P, KD, D])
        ident = sb("ident", [P, P])
        minus_half = sb("minus_half", [P, 2 * GH * STEPS])
        iota8 = sb("iota8", [P, E])

        xin = sb("xin", [P, 2, KP, P])
        h_all = sb("h_all", [P, TILES, D])
        xn = sb("xn", [P, D])
        xT = sb("xT", [P, KD, P])
        qkvg = sb("qkvg", [P, HG * GC])
        rin = sb("rin", [P, 2, STEPS, GC])
        sq = sb("sq", [P, STEPS, 2 * GW])
        n2 = sb("n2", [P, STEPS, 2, GH])
        n2c = sb("n2c", [P, STEPS, 2, GH])
        inv = sb("inv", [P, STEPS, 2, GH])
        gz = sb("gz", [P, STEPS, 2 * GH])
        gt = sb("gt", [P, STEPS, 2 * GH])
        gates = sb("gates", [P, 2, STEPS, 2, GH])
        ia = sb("ia", [P, 2, STEPS, 2, GH])
        iab = sb("iab", [P, STEPS, GH])
        vb = sb("vb", [P, 2, STEPS, GW])
        pq = sb("pq", [P, STEPS, GH, DH])
        kqr = sb("kqr", [P, STEPS, GH])
        kq = sb("kq", [P, 2, STEPS, GH])
        S = sb("S", [P, 2, GH, DH, DH])
        prod = sb("prod", [P, GH, DH, DH])
        rsum = sb("rsum", [P, GW])
        ub = sb("ub", [P, STEPS, GW])
        outer = sb("outer", [P, GH, DH, DH])
        qprod = sb("qprod", [P, GH, DH, DH])
        tree8 = sb("tree8", [P, GH * DH, 8])
        tree4 = sb("tree4", [P, GH * DH, 4])
        tree2 = sb("tree2", [P, GH * DH, 2])
        oq = sb("oq", [P, STEPS, GW])
        o1 = sb("o1", [P, STEPS, GW])
        o2 = sb("o2", [P, STEPS, GW])
        og = sb("og", [P, STEPS, GW])
        otok = sb("otok", [P, D])
        oT = sb("oT", [P, KD, P])
        h1 = sb("h1", [P, 2, D])
        x2n = sb("x2n", [P, D])
        x2T = sb("x2T", [P, 2, KD, P])
        stat = sb("stat", [P, 2, 6])
        mv = sb("mv", [P, 2, 2])
        veps = sb("veps", [P, 2, 1])
        rstd = sb("rstd", [P, 2, 1])
        carrier = sb("carrier", [P, 1])
        lg = sb("lg", [P, E + 1])
        top8 = sb("top8", [P, 8])
        topi = sb("topi", [P, 8], U32)
        topf = sb("topf", [P, 8])
        z9 = sb("z9", [P, E + 1])
        t9 = sb("t9", [P, E + 1])
        num = sb("num", [P, E])
        den = sb("den", [P, E])
        rden = sb("rden", [P, E])
        ex = sb("ex", [P, E])
        esum = sb("esum", [P, 1])
        rsm = sb("rsm", [P, 1])
        mask1 = sb("mask1", [P, E])
        mask2 = sb("mask2", [P, E])
        comb = sb("comb", [P, 2, E + 1])
        hs = sb("hs", [P, 4, 2, KD, P])
        sg = sb("sg", [P, KD, P])
        hsh = sb("hsh", [P, KD, P])
        acc = sb("acc", [P, 2, D])

        qkvg_dram = nc.dram_tensor("qkvg_dram", [2, P, HG * GC], F32).ap()
        o_dram = nc.dram_tensor("o_dram", [2, P, STEPS * GW], F32).ap()

        bank = [ctx.enter_context(nc.psum_tensor(f"bank{i}", [P, BANK], F32)) for i in range(4)]
        kk = ctx.enter_context(nc.psum_tensor("kk", [P, 2, 2, STEPS, GH, DH], F32))
        decayed = ctx.enter_context(nc.psum_tensor("decayed", [P, GH, DH, DH], F32))

        ld_patch, ld_attn, ld_txt, ld_router, ld_up, ld_down, ld_shared = (
            sem(n) for n in ("ld_patch", "ld_attn", "ld_txt", "ld_router", "ld_up", "ld_down", "ld_shared"))
        xin_in, rin_in, otok_in, acc_free, qkvg_out, o_out = (
            [sem(f"{n}{k}") for k in range(2)]
            for n in ("xin_in", "rin_in", "otok_in", "acc_free", "qkvg_out", "o_out"))
        const_ready = sem("const_ready")
        pe_h, pe_xT, pe_qkv, pe_oT, pe_wout, pe_x2T, pe_router, pe_up, pe_gu, pe_down = (
            sem(n) for n in ("pe_h", "pe_xT", "pe_qkv", "pe_oT", "pe_wout", "pe_x2T", "pe_router", "pe_up", "pe_gu",
                             "pe_down"))
        act_h, act_xT, act_qkv, act_oT, act_x2T, act_hs, act_sg, act_sq, act_gt, act_t9, act_decay = (
            sem(n) for n in ("act_h", "act_xT", "act_qkv", "act_oT", "act_x2T", "act_hs", "act_sg", "act_sq",
                             "act_gt", "act_t9", "act_decay"))
        pool_rstd1, pool_rstd2, pool_inv, pool_qprod, pool_tree, pool_oq = (
            sem(n) for n in ("pool_rstd1", "pool_rstd2", "pool_inv", "pool_qprod", "pool_tree", "pool_oq"))
        (dve_st1, dve_st2, dve_xn, dve_x2n, dve_h1, dve_gz, dve_n2, dve_n2c, dve_gates, dve_prep, dve_prod, dve_rsum,
         dve_u, dve_outer, dve_state, dve_o12, dve_o, dve_logits, dve_z9, dve_route, dve_comb, dve_acc,
         dve_gu, dve_gsum) = (
            sem(n) for n in ("dve_st1", "dve_st2", "dve_xn", "dve_x2n", "dve_h1", "dve_gz", "dve_n2", "dve_n2c",
                             "dve_gates", "dve_prep", "dve_prod", "dve_rsum", "dve_u", "dve_outer", "dve_state",
                             "dve_o12", "dve_o", "dve_logits", "dve_z9", "dve_route", "dve_comb", "dve_acc",
                             "dve_gu", "dve_gsum"))

        block = ctx.enter_context(nc.Block())

        def stages(i):
            return {"A": 0 <= i + 2 < TILES, "patch": 0 <= i + 2 < PATCH_TILES, "B": 0 <= i + 1 < TILES,
                    "R": 0 <= i < TILES, "O": 0 <= i - 1 < TILES, "M": 0 <= i - 2 < TILES}

        FIRST, LAST = -2, TILES + 1

        def run(eng, body):
            def peeled(first, last):
                for i in range(first, last):
                    body(i, i % 2, stages(i), lambda off: (i + off) // 2)

            def pairs(first, last):
                with eng.Fori(0, (last - first) // 2) as pair:
                    for n in range(2):
                        c = first + n
                        body(pair * 2 + c, c % 2, stages(c), lambda off: pair + (c + off) // 2)

            peeled(FIRST, 3)
            pairs(3, PATCH_TILES - 2)
            pairs(PATCH_TILES - 2, TILES - 2)
            peeled(TILES - 2, LAST + 1)

        bank_order = [
            [("x2T", "M", -2, act_x2T, 1, 1), ("oT", "O", -1, act_oT, 1, 1), ("xT", "A", 2, act_xT, 1, 1),
             ("qkv0", "A", 2, act_qkv, 2, 1), ("gu", "M", -2, dve_gu, 1, 1)],
            [("h", "patch", 2, act_h, 1, 1), ("up1", "M", -2, act_hs, 4, 2), ("up2", "M", -2, act_hs, 4, 3),
             ("up3", "M", -2, act_hs, 4, 4)],
            [("router", "M", -2, dve_logits, 1, 1), ("down0", "M", -2, dve_acc, 5, 1),
             ("down1", "M", -2, dve_acc, 5, 2), ("down2", "M", -2, dve_acc, 5, 3), ("downS", "M", -2, dve_acc, 5, 5)],
            [("up0", "M", -2, act_hs, 4, 1), ("wout", "O", -1, dve_h1, 1, 1), ("qkv1", "A", 2, act_qkv, 2, 2),
             ("down3", "M", -2, dve_acc, 5, 4)],
        ]
        bank_of = {group[0]: n for n, order in enumerate(bank_order) for group in order}

        def take(pe, name, i, st, before):
            for b, order in enumerate(bank_order):
                names = [g[0] for g in order]
                if name in names:
                    at = names.index(name)
                    back = [(g, 0, st) for g in reversed(order[:at])] + [(g, -1, before) for g in reversed(order)]
                    for (_, stage, off, s, per, nth), turn, live in back:
                        if live[stage]:
                            pe.wait_ge(s, (i + (off + turn)) * per + nth)
                            break
                    return bank[b]

        @block.sync
        def _(sp):
            sp.dma_start(wp[:], w_patch).then_inc(ld_patch, 16)
            sp.dma_start(pbias[:], patch_bias).then_inc(ld_patch, 16)
            sp.dma_start(sel[:], selector).then_inc(ld_patch, 16)
            sp.dma_start(xin[:, 0], patches[0]).then_inc(xin_in[0], 16)
            sp.dma_start(ident[:], identity).then_inc(ld_attn, 16)
            sp.dma_start(wq[:], w_qkvg).then_inc(ld_attn, 16)
            sp.dma_start(gbias[:], gate_bias).then_inc(ld_attn, 16)
            sp.dma_start(wo[:], w_out).then_inc(ld_attn, 16)
            sp.dma_start(wr[:], w_router).then_inc(ld_router, 16)
            sp.dma_start(wu[:], w_up).then_inc(ld_up, 16)
            sp.dma_start(wd[:], w_down).then_inc(ld_down, 16)
            sp.dma_start(wsu[:], w_shared_up).then_inc(ld_shared, 16)
            sp.dma_start(wsd[:], w_shared_down).then_inc(ld_shared, 16)
            sp.dma_start(h_all[:, PATCH_TILES:TILES], txt).then_inc(ld_txt, 16)

            def body(i, par, st, half):
                if st["patch"]:
                    if not isinstance(i, int) or i > FIRST:
                        sp.wait_ge(pe_h, i + 2)
                    sp.dma_start(xin[:, 1 - par], patches[i + 3]).then_inc(xin_in[1 - par], 16)
                if st["A"]:
                    sp.wait_ge(act_qkv, (i + 3) * 2)
                    sp.dma_start(qkvg_dram[par], qkvg[:]).then_inc(qkvg_out[par], 16)
                if st["R"]:
                    sp.wait_ge(dve_o, i + 1)
                    sp.dma_start(o_dram[par], og[:]).then_inc(o_out[par], 16)
                if st["A"]:
                    sp.wait_ge(qkvg_out[par], (half(2) + 1) * 16)
                    for g in range(HG):
                        sp.dma_start(rin[g * B:(g + 1) * B, par],
                                     qkvg_dram[par, :, g * GC:(g + 1) * GC].rearrange("(s b) c -> b s c", s=STEPS))\
                          .then_inc(rin_in[par], 16)
                if st["R"]:
                    sp.wait_ge(o_out[par], (half(0) + 1) * 16)
                    for s in range(STEPS):
                        sp.dma_start(otok[s * B:(s + 1) * B],
                                     o_dram[par, :, s * GW:(s + 1) * GW].rearrange("(g b) c -> b g c", g=HG))\
                          .then_inc(otok_in[par], 16)
                if st["M"]:
                    sp.wait_ge(dve_acc, (i - 1) * 5)
                    sp.dma_start(out[i - 2], acc[:, par]).then_inc(acc_free[par], 16)

            run(sp, body)
            for k in range(2):
                sp.wait_ge(acc_free[k], 16 + 16 * ((TILES + 1 - k) // 2))

        @block.tensor
        def _(pe):
            def matmuls(dst, pairs, done=None):
                for n, (l, r) in enumerate(pairs):
                    mm = pe.matmul(dst, l, r, start=(n == 0), stop=(n == len(pairs) - 1))
                if done is not None:
                    mm.then_inc(done, 1)

            def body(i, par, st, half):
                before = stages(i - 1) if isinstance(i, int) else st
                first = isinstance(i, int) and i == FIRST

                def up(k):
                    dst = take(pe, f"up{k}", i, st, before)
                    if isinstance(i, int) and i == 2:
                        pe.wait_ge(ld_up, 16)
                    for e in range(2):
                        for f in range(KD):
                            c = (e * KD + f) * P
                            matmuls(dst[:, c:c + P],
                                    [(wu[:, 2 * k + e, d, f * P:(f + 1) * P], x2T[:, par, d, :]) for d in range(KD)],
                                    pe_up if (e, f) == (1, KD - 1) else None)

                def down(k):
                    dst = take(pe, f"down{k}", i, st, before)
                    if isinstance(i, int) and i == 2:
                        pe.wait_ge(ld_down, 16)
                    pe.wait_ge(act_hs, (i - 2) * 4 + k + 1)
                    for e in range(2):
                        matmuls(dst[:, e * D:(e + 1) * D],
                                [(hs[:, k, e, f, :], wd[:, 2 * k + e, f, :]) for f in range(KD)],
                                pe_down if e else None)

                def turned(name, s, src):
                    dst = take(pe, name, i, st, before)
                    for d in range(KD):
                        tr = pe.transpose(dst[:, d * P:(d + 1) * P], src[:, d * P:(d + 1) * P], ident[:])
                    tr.then_inc(s, 1)

                if st["M"]:
                    pe.wait_ge(dve_x2n, i - 1)
                    turned("x2T", pe_x2T, x2n)
                if st["patch"]:
                    dst = take(pe, "h", i, st, before)
                    if first:
                        pe.wait_ge(ld_patch, 48)
                    pe.wait_ge(xin_in[par], (half(2) + 1) * 16)
                    pe.matmul(dst[:, 0:D], sel[:], pbias[:, i + 2, :], start=True, stop=False)
                    for d in range(KP):
                        mm = pe.matmul(dst[:, 0:D], xin[:, par, d, :], wp[:, d, :], start=False, stop=(d == KP - 1))
                    mm.then_inc(pe_h, 1)
                if st["M"]:
                    dst = take(pe, "router", i, st, before)
                    if isinstance(i, int) and i == 2:
                        pe.wait_ge(ld_router, 16)
                    pe.wait_ge(act_x2T, i - 1)
                    matmuls(dst[:, 0:E + 1], [(x2T[:, par, d, :], wr[:, d, :]) for d in range(KD)], pe_router)
                    up(0)
                if st["O"]:
                    pe.wait_ge(otok_in[1 - par], (half(-1) + 1) * MOVES)
                    turned("oT", pe_oT, otok)
                if st["M"]:
                    up(1)
                    down(0)
                if st["O"]:
                    dst = take(pe, "wout", i, st, before)
                    pe.wait_ge(act_oT, i)
                    matmuls(dst[:, 0:D], [(oT[:, d, :], wo[:, d, :]) for d in range(KD)], pe_wout)
                if st["A"]:
                    if first:
                        pe.wait_ge(ld_attn, 64)
                    pe.wait_ge(dve_xn, i + 3)
                    turned("xT", pe_xT, xn)
                if st["M"]:
                    up(2)
                    down(1)
                if st["A"]:
                    pe.wait_ge(act_xT, i + 3)
                    cols = HG * GC // 2
                    for n in range(2):
                        dst = take(pe, f"qkv{n}", i, st, before)
                        matmuls(dst[:, 0:cols], [(xT[:, d, :], wq[:, d, n * cols:(n + 1) * cols]) for d in range(KD)],
                                pe_qkv)
                if st["M"]:
                    up(3)
                    down(2)
                    dst = take(pe, "gu", i, st, before)
                    if isinstance(i, int) and i == 2:
                        pe.wait_ge(ld_shared, 32)
                    for f in range(2 * KD):
                        matmuls(dst[:, f * P:(f + 1) * P],
                                [(wsu[:, d, f * P:(f + 1) * P], x2T[:, par, d, :]) for d in range(KD)],
                                pe_gu if f == 2 * KD - 1 else None)
                    down(3)
                    dst = take(pe, "downS", i, st, before)
                    pe.wait_ge(dve_gu, i - 1)
                    matmuls(dst[:, 0:D], [(hsh[:, f, :], wsd[:, f, :]) for f in range(KD)], pe_down)

            run(pe, body)

        @block.scalar
        def _(act):
            act.preload_act_table_set("silu_and_others")

            def body(i, par, st, half):
                def decay(s):
                    act.wait_ge(dve_state, i * STEPS + s + 1)
                    if s == 0:
                        act.wait_ge(dve_gates, i + 1)
                    for g in range(GH):
                        act.activation(decayed[:, g], S[:, (s + 1) % 2, g], ACT.Copy,
                                       scale=gates[:, par, s, 0, g:g + 1]).then_inc(act_decay, 1)

                def hidden(k):
                    act.wait_ge(pe_up, (i - 2) * 4 + k + 1)
                    if not isinstance(i, int) or i >= 3:
                        act.wait_ge(pe_down, (i - 3) * 5 + k + 1)
                    act.activation(hs[:, k].rearrange("p e f t -> p (e f t)"), bank[bank_of[f"up{k}"]][:], ACT.Silu)\
                       .then_inc(act_hs, 1)

                def evacuate(name, dst, waited, count, done):
                    act.wait_ge(waited, count)
                    act.activation(dst, bank[bank_of[name]][:, 0:D], ACT.Copy).then_inc(done, 1)

                if st["R"]:
                    decay(0)
                if st["M"]:
                    evacuate("x2T", x2T[:, par].rearrange("p d t -> p (d t)"), pe_x2T, i - 1, act_x2T)
                if st["patch"]:
                    evacuate("h", h_all[:, i + 2, :], pe_h, i + 3, act_h)
                if st["B"]:
                    act.wait_ge(rin_in[1 - par], (half(1) + 1) * MOVES)
                    if not isinstance(i, int) or i >= 0:
                        act.wait_ge(dve_n2, i + 1)
                    act.activation(sq[:], rin[:, 1 - par, :, 0:2 * GW], ACT.Square).then_inc(act_sq, 1)
                if st["M"]:
                    act.wait_ge(dve_z9, (i - 1) * 2)
                    act.activation(t9[:], z9[:], ACT.Tanh, scale=0.5).then_inc(act_t9, 1)
                    hidden(0)
                if st["O"]:
                    evacuate("oT", oT[:].rearrange("p d t -> p (d t)"), pe_oT, i, act_oT)
                if st["M"]:
                    hidden(1)
                if st["R"]:
                    decay(1)
                if st["B"]:
                    act.wait_ge(dve_gz, i + 2)
                    act.activation(gt[:], gz[:], ACT.Tanh, scale=0.5).then_inc(act_gt, 1)
                if st["A"]:
                    evacuate("xT", xT[:].rearrange("p d t -> p (d t)"), pe_xT, i + 3, act_xT)
                if st["M"]:
                    hidden(2)
                if st["R"]:
                    decay(2)
                if st["A"]:
                    cols = HG * GC // 2
                    for n in range(2):
                        act.wait_ge(pe_qkv, (i + 2) * 2 + n + 1)
                        if n == 0 and (not isinstance(i, int) or i > FIRST):
                            act.wait_ge(qkvg_out[1 - par], (half(1) + 1) * 16)
                        act.activation(qkvg[:, n * cols:(n + 1) * cols], bank[bank_of[f"qkv{n}"]][:, 0:cols],
                                       ACT.Copy).then_inc(act_qkv, 1)
                if st["M"]:
                    hidden(3)
                    act.wait_ge(pe_gu, i - 1)
                    if not isinstance(i, int) or i >= 3:
                        act.wait_ge(dve_gu, i - 2)
                    act.activation(sg[:].rearrange("p f t -> p (f t)"), bank[bank_of["gu"]][:, 0:F], ACT.Silu)\
                       .then_inc(act_sg, 1)
                if st["R"]:
                    decay(3)

            run(act, body)

        @block.gpsimd
        def _(pool):
            pool.memset(minus_half[:], -0.5).then_inc(const_ready, 1)
            pool.iota(topi[:], pattern=[[1, 8]], base=0, channel_multiplier=0).then_inc(const_ready, 1)
            pool.wait_ge(const_ready, 2)
            pool.tensor_copy(iota8[:], topi[:]).then_inc(const_ready, 1)
            pool.wait_ge(const_ready, 3)

            def body(i, par, st, half):
                def read_out(s):
                    pool.wait_ge(dve_state, i * STEPS + s + 1)
                    q = rin[:, par, s, 0:GW].rearrange("p (h d) -> p h d", h=GH)
                    pool.tensor_tensor(qprod[:], S[:, (s + 1) % 2], q.unsqueeze(2).to_broadcast([P, GH, DH, DH]),
                                       ALU.mult).then_inc(pool_qprod, 1)
                    at = i * STEPS + s
                    qrows = qprod[:].rearrange("p h r d -> p (h r) d")
                    pool.wait_ge(pool_qprod, at + 1)
                    pool.tensor_tensor(tree8[:], qrows[:, :, 0:8], qrows[:, :, 8:16], ALU.add).then_inc(pool_tree, 1)
                    pool.wait_ge(pool_tree, at * 3 + 1)
                    pool.tensor_tensor(tree4[:], tree8[:, :, 0:4], tree8[:, :, 4:8], ALU.add).then_inc(pool_tree, 1)
                    pool.wait_ge(pool_tree, at * 3 + 2)
                    pool.tensor_tensor(tree2[:], tree4[:, :, 0:2], tree4[:, :, 2:4], ALU.add).then_inc(pool_tree, 1)
                    pool.wait_ge(pool_tree, at * 3 + 3)
                    if s == 0 and (not isinstance(i, int) or i >= 1):
                        pool.wait_ge(dve_o12, i * 2)
                    pool.tensor_tensor(oq[:, s, :], tree2[:, :, 0], tree2[:, :, 1], ALU.add).then_inc(pool_oq, 1)

                if st["R"]:
                    read_out(0)
                if st["A"]:
                    pool.wait_ge(dve_st1, (i + 3) * 3)
                    pool.tensor_tensor(rstd[:, 0], veps[:, 0], minus_half[:, 0:1], ALU.pow).then_inc(pool_rstd1, 1)
                if st["R"]:
                    read_out(1)
                if st["B"]:
                    pool.wait_ge(dve_n2c, i + 2)
                    pool.tensor_tensor(inv[:].rearrange("p s k h -> p (s k h)"),
                                       n2c[:].rearrange("p s k h -> p (s k h)"), minus_half[:],
                                       ALU.pow).then_inc(pool_inv, 1)
                if st["O"]:
                    pool.wait_ge(dve_st2, i * 3)
                    pool.tensor_tensor(rstd[:, 1], veps[:, 1], minus_half[:, 0:1], ALU.pow).then_inc(pool_rstd2, 1)
                if st["R"]:
                    read_out(2)
                    read_out(3)

            run(pool, body)

        @block.vector
        def _(dve):
            PREP, ROUTE = 9, 12
            dve.memset(S[:, 1], 0.0).then_inc(dve_state, 1)
            for k in range(2):
                dve.memset(acc[:, k], 0.0).then_inc(acc_free[k], 16)
            dve.wait_ge(const_ready, 3)

            def body(i, par, st, half):
                inner = not isinstance(i, int)

                def statistics(which, src, s, tile):
                    dve.bn_stats(stat[:, which], src).then_inc(s, 1)
                    dve.wait_ge(s, tile * 3 + 1)
                    dve.memset(carrier[:], 0.0)
                    dve.bn_aggr(mv[:, which], stat[:, which]).then_inc(s, 1)
                    dve.wait_ge(s, tile * 3 + 2)
                    dve.tensor_scalar(veps[:, which], mv[:, which, 1:2], EPS_LN, None, ALU.add).then_inc(s, 1)

                def residual():
                    dve.wait_ge(pe_wout, i)
                    dve.tensor_tensor(h1[:, 1 - par], bank[bank_of["wout"]][:, 0:D], h_all[:, i - 1, :], ALU.add)\
                       .then_inc(dve_h1, 1)
                    dve.wait_ge(dve_h1, i)
                    statistics(1, h1[:, 1 - par], dve_st2, i - 1)

                def norm_1_statistics():
                    if st["patch"]:
                        dve.wait_ge(act_h, i + 3)
                    else:
                        dve.wait_ge(ld_txt, 16)
                    statistics(0, h_all[:, i + 2, :], dve_st1, i + 2)

                def norm_2():
                    dve.wait_ge(pool_rstd2, i)
                    if inner or i >= 2:
                        dve.wait_ge(pe_x2T, i - 1)
                    dve.tensor_scalar(x2n[:], h1[:, 1 - par], mv[:, 1, 0:1], rstd[:, 1], ALU.subtract, ALU.mult)\
                       .then_inc(dve_x2n, 1)

                def norm_1():
                    dve.wait_ge(pool_rstd1, i + 3)
                    if inner or i >= -1:
                        dve.wait_ge(pe_xT, i + 2)
                    dve.tensor_scalar(xn[:], h_all[:, i + 2, :], mv[:, 0, 0:1], rstd[:, 0], ALU.subtract, ALU.mult)\
                       .then_inc(dve_xn, 1)

                def add_experts(k):
                    dve.wait_ge(pe_down, (i - 2) * 5 + k + 1)
                    if k == 0:
                        dve.wait_ge(acc_free[par], (half(-2) + 1) * 16)
                    for e in ([0, 1] if k < 4 else [0]):
                        src = h1[:, par] if (k, e) == (0, 0) else acc[:, par]
                        n = 2 * k + e
                        if (k, e) != (0, 0):
                            if e == 1:
                                dve.wait_ge(dve_gsum, (i - 2) * 4 + k + 1)
                            else:
                                dve.wait_ge(dve_acc, (i - 2) * 5 + k)
                        ins = dve.scalar_tensor_tensor(acc[:, par], bank[bank_of[f"down{k}" if k < 4 else "downS"]][:, e * D:(e + 1) * D],
                                                       comb[:, par, n:n + 1], src, ALU.mult, ALU.add)
                        ins.then_inc(dve_gsum if (e == 0 and k < 4) else dve_acc, 1)

                def gated_up():
                    dve.wait_ge(act_sg, i - 1)
                    if inner or i >= 3:
                        dve.wait_ge(pe_down, (i - 2) * 5)
                    dve.tensor_tensor(hsh[:].rearrange("p f t -> p (f t)"), bank[bank_of["gu"]][:, F:2 * F],
                                      sg[:].rearrange("p f t -> p (f t)"), ALU.mult).then_inc(dve_gu, 1)

                def gate_inputs():
                    dve.wait_ge(rin_in[1 - par], (half(1) + 1) * MOVES)
                    if not inner and i == -1:
                        dve.wait_ge(ld_attn, 64)
                    dve.tensor_tensor(gz[:], rin[:, 1 - par, :, 3 * GW:GC],
                                      gbias[:].unsqueeze(1).to_broadcast([P, STEPS, 2 * GH]), ALU.add)\
                       .then_inc(dve_gz, 1)

                def norms():
                    dve.wait_ge(act_sq, i + 2)
                    dve.tensor_reduce(n2[:].rearrange("p s k h -> p s (k h)"),
                                      sq[:].rearrange("p s (m d) -> p s m d", d=DH), AX.X, ALU.add).then_inc(dve_n2, 1)
                    dve.wait_ge(dve_n2, i + 2)
                    dve.tensor_scalar(n2c[:], n2[:], EPS_N2, None, ALU.max).then_inc(dve_n2c, 1)

                def gate_values():
                    dve.wait_ge(act_gt, i + 2)
                    dve.tensor_scalar(gates[:, 1 - par].rearrange("p s k h -> p s (k h)"), gt[:], 0.5, 0.5, ALU.mult,
                                      ALU.add).then_inc(dve_gates, 1)

                def heads(ap):
                    return ap.rearrange("p s (h d) -> p s h d", h=GH)

                def over_width(ap):
                    return ap.unsqueeze(3).to_broadcast([P, STEPS, GH, DH])


                q, k, v = (heads(rin[:, 1 - par, :, n * GW:(n + 1) * GW]) for n in range(3))
                prep = (i + 1) * PREP

                def prepare_k():
                    dve.wait_ge(pool_inv, i + 2)
                    dve.wait_ge(dve_gates, i + 2)
                    for n in range(2):
                        dve.tensor_tensor(ia[:, 1 - par, :, n, :], inv[:, :, n, :], gates[:, 1 - par, :, 0, :],
                                          ALU.mult).then_inc(dve_prep, 1)
                    dve.tensor_tensor(kk[:, 1 - par, 0], k, over_width(inv[:, :, 1, :]), ALU.mult).then_inc(dve_prep, 1)
                    dve.wait_ge(dve_prep, prep + 2)
                    dve.tensor_tensor(iab[:], ia[:, 1 - par, :, 1, :], gates[:, 1 - par, :, 1, :], ALU.mult)\
                       .then_inc(dve_prep, 1)
                    dve.tensor_tensor(heads(vb[:, 1 - par]), v, over_width(gates[:, 1 - par, :, 1, :]), ALU.mult)\
                       .then_inc(dve_prep, 1)

                def prepare_products():
                    dve.wait_ge(dve_prep, prep + 4)
                    dve.tensor_tensor(kk[:, 1 - par, 1], k, over_width(iab[:]), ALU.mult).then_inc(dve_prep, 1)
                    dve.tensor_tensor(pq[:], kk[:, 1 - par, 0], q, ALU.mult).then_inc(dve_prep, 1)

                def prepare_kq():
                    dve.wait_ge(dve_prep, prep + 7)
                    dve.tensor_reduce(kqr[:], pq[:], AX.X, ALU.add).then_inc(dve_prep, 1)
                    dve.wait_ge(dve_prep, prep + 8)
                    dve.tensor_tensor(kq[:, 1 - par], kqr[:], inv[:, :, 0, :], ALU.mult).then_inc(dve_prep, 1)

                def step(s, fill):
                    t = i * STEPS + s
                    old, new = S[:, (s + 1) % 2], S[:, s % 2]
                    shape = [P, GH, DH, DH]
                    dve.wait_ge(dve_state, t + 1)
                    if s == 0:
                        dve.wait_ge(dve_prep, (i + 1) * PREP)
                    dve.tensor_tensor(prod[:], old, kk[:, par, 1, s].unsqueeze(2).to_broadcast(shape), ALU.mult)\
                       .then_inc(dve_prod, 1)
                    fill()
                    dve.wait_ge(dve_prod, t + 1)
                    dve.tensor_reduce(rsum[:].rearrange("p (h r) -> p h r", h=GH), prod[:], AX.X, ALU.add)\
                       .then_inc(dve_rsum, 1)
                    fill()
                    dve.wait_ge(dve_rsum, t + 1)
                    dve.tensor_tensor(ub[:, s, :], vb[:, par, s, :], rsum[:], ALU.subtract).then_inc(dve_u, 1)
                    dve.wait_ge(dve_u, t + 1)
                    u = ub[:, s, :].rearrange("p (h r) -> p h r", h=GH)
                    dve.tensor_tensor(outer[:], u.unsqueeze(3).to_broadcast(shape),
                                      kk[:, par, 0, s].unsqueeze(2).to_broadcast(shape), ALU.mult)\
                       .then_inc(dve_outer, 1)
                    fill()
                    dve.wait_ge(dve_outer, t + 1)
                    dve.wait_ge(act_decay, (t + 1) * GH)
                    if inner or i >= 1 or s >= 1:
                        dve.wait_ge(pool_qprod, t)
                    dve.tensor_tensor(new, decayed[:], outer[:], ALU.add).then_inc(dve_state, 1)
                    fill()

                def head_outputs():
                    dve.wait_ge(pool_oq, (i + 1) * STEPS)
                    dve.tensor_tensor(heads(o1[:]), heads(oq[:]), over_width(ia[:, par, :, 0, :]), ALU.mult)\
                       .then_inc(dve_o12, 1)
                    dve.tensor_tensor(heads(o2[:]), heads(ub[:]), over_width(kq[:, par]), ALU.mult).then_inc(dve_o12, 1)
                    dve.wait_ge(dve_o12, (i + 1) * 2)
                    if inner or i >= 1:
                        dve.wait_ge(o_out[1 - par], (half(-1) + 1) * 16)
                    dve.tensor_tensor(og[:], o1[:], o2[:], ALU.add).then_inc(dve_o, 1)

                def route_inputs():
                    dve.wait_ge(pe_router, i - 1)
                    dve.tensor_copy(lg[:], bank[bank_of["router"]][:, 0:E + 1]).then_inc(dve_logits, 1)
                    dve.wait_ge(dve_logits, i - 1)
                    dve.tensor_copy(z9[:, E:E + 1], lg[:, E:E + 1]).then_inc(dve_z9, 1)
                    dve.max(top8[:], lg[:, 0:E]).then_inc(dve_route, 1)
                    at = (i - 2) * ROUTE
                    dve.wait_ge(dve_route, at + 1)
                    dve.tensor_scalar(z9[:, 0:E], lg[:, 0:E], top8[:, 0:1], None, ALU.subtract).then_inc(dve_z9, 1)
                    dve.max_index(topi[:], top8[:], lg[:, 0:E]).then_inc(dve_route, 1)
                    dve.wait_ge(dve_route, at + 2)
                    dve.tensor_copy(topf[:], topi[:]).then_inc(dve_route, 1)
                    dve.wait_ge(dve_route, at + 3)
                    dve.tensor_scalar(mask1[:], iota8[:], topf[:, 0:1], None, ALU.is_equal).then_inc(dve_route, 1)
                    dve.wait_ge(dve_route, at + 4)
                    dve.scalar_tensor_tensor(mask2[:], iota8[:], topf[:, 1:2], mask1[:], ALU.is_equal, ALU.add)\
                       .then_inc(dve_route, 1)

                def route_weights():
                    at = (i - 2) * ROUTE
                    dve.wait_ge(act_t9, i - 1)
                    dve.tensor_scalar(den[:], t9[:, 0:E], -1.0, 1.0, ALU.mult, ALU.add).then_inc(dve_route, 1)
                    dve.tensor_scalar(num[:], t9[:, 0:E], 1.0, None, ALU.add).then_inc(dve_route, 1)
                    dve.tensor_scalar(comb[:, par, E:E + 1], t9[:, E:E + 1], 0.5, 0.5, ALU.mult, ALU.add)\
                       .then_inc(dve_route, 1)
                    dve.wait_ge(dve_route, at + 8)
                    dve.reciprocal(rden[:], den[:]).then_inc(dve_route, 1)
                    dve.wait_ge(dve_route, at + 9)
                    dve.tensor_tensor(ex[:], num[:], rden[:], ALU.mult).then_inc(dve_route, 1)
                    dve.wait_ge(dve_route, at + 10)
                    dve.tensor_reduce(esum[:], ex[:], AX.X, ALU.add).then_inc(dve_route, 1)
                    dve.wait_ge(dve_route, at + 11)
                    dve.reciprocal(rsm[:], esum[:]).then_inc(dve_route, 1)
                    dve.wait_ge(dve_route, at + 12)
                    dve.scalar_tensor_tensor(comb[:, par, 0:E], ex[:], rsm[:], mask2[:], ALU.mult, ALU.mult)\
                       .then_inc(dve_comb, 1)

                fills = {(s, n): [] for s in range(STEPS) for n in range(4)}
                if st["M"]:
                    fills[0, 0] += [route_inputs]
                    fills[0, 2] += [route_weights]
                    fills[0, 3] += [lambda: dve.wait_ge(dve_comb, i - 1), lambda: add_experts(0)]
                    fills[1, 3] += [lambda: add_experts(1)]
                    fills[2, 2] += [lambda: add_experts(2)]
                    fills[3, 0] += [gated_up]
                    fills[3, 2] += [lambda: add_experts(3)]
                    fills[3, 3] += [lambda: add_experts(4)]
                if st["A"]:
                    fills[0, 1] += [norm_1_statistics]
                    fills[1, 1] += [norm_1]
                if st["B"]:
                    fills[1, 0] += [gate_inputs, norms]
                    fills[2, 0] += [gate_values]
                    fills[2, 1] += [prepare_k]
                    fills[2, 3] += [prepare_products]
                    fills[3, 1] += [prepare_kq]
                if st["O"]:
                    fills[1, 2] += [residual]
                    fills[3, 0] += [norm_2]
                for s in range(STEPS):
                    if st["R"]:
                        turn = iter(range(4))

                        def fill(s=s, turn=turn):
                            for part in fills[s, next(turn)]:
                                part()
                        step(s, fill)
                    else:
                        for n in range(4):
                            for part in fills[s, n]:
                                part()
                if st["R"]:
                    head_outputs()

            run(dve, body)


def kernel(x, txt, L0_tok_W, L0_tok_b, L0_tok_pos_embd, L0_attn_Wqkv, L0_attn_Wg, L0_attn_bg, L0_attn_Wb, L0_attn_bb,
           L0_attn_Wout, L0_ffn_router_w, L0_ffn_w1, L0_ffn_w2, L0_ffn_shared_gate_up, L0_ffn_shared_down,
           L0_ffn_shared_gate_w):
    import numpy as np
    import concourse.bacc as bacc
    from concourse.bass_utils import run_bass_kernel_spmd

    def a(v):
        return np.asarray(v)

    def blocked(w):
        return a(w).reshape(-1, P, w.shape[-1]).transpose(1, 0, 2)

    side = int(PATCHES ** 0.5)
    px = x.shape[-1] // side
    patches = a(x).reshape(B, 3, side, px, side, px).transpose(2, 4, 1, 3, 5, 0)
    patches = patches.reshape(PATCH_TILES, STEPS, KP, P, B).transpose(0, 3, 2, 1, 4)
    text = a(txt).transpose(1, 0, 2).reshape(TILES - PATCH_TILES, P, D).transpose(1, 0, 2)
    pos = a(L0_tok_pos_embd).reshape(PATCH_TILES, STEPS, D).transpose(1, 0, 2)
    bias = np.broadcast_to(a(L0_tok_b), (1, PATCH_TILES, D))
    qkv = a(L0_attn_Wqkv).reshape(3, HG, GW, D)
    gates = np.stack([a(L0_attn_Wg), a(L0_attn_Wb)]).reshape(2, HG, GH, D)
    w_qkvg = np.concatenate([np.concatenate([*qkv[:, g], *gates[:, g]]) for g in range(HG)]).T
    gate_bias = np.concatenate([a(L0_attn_bg).reshape(HG, GH), a(L0_attn_bb).reshape(HG, GH)], axis=1)
    selector = np.concatenate([np.repeat(np.eye(STEPS), B, axis=1), np.ones((1, P))]).astype(np.float32)
    ins = {
        "patches": np.concatenate([patches, patches[-1:]]).reshape(PATCH_TILES + 1, P, KP, P),
        "txt": text,
        "w_patch": blocked(a(L0_tok_W).T),
        "patch_bias": np.concatenate([pos, bias]),
        "w_qkvg": blocked(w_qkvg),
        "gate_bias": np.repeat(gate_bias, B, axis=0),
        "w_out": blocked(a(L0_attn_Wout).T),
        "w_router": blocked(np.concatenate([a(L0_ffn_router_w), a(L0_ffn_shared_gate_w)], axis=1)),
        "w_up": a(L0_ffn_w1).reshape(E, KD, P, F).transpose(2, 0, 1, 3),
        "w_down": a(L0_ffn_w2).reshape(E, KD, P, D).transpose(2, 0, 1, 3),
        "w_shared_up": blocked(L0_ffn_shared_gate_up),
        "w_shared_down": blocked(L0_ffn_shared_down),
        "selector": selector,
        "identity": np.eye(P, dtype=np.float32),
    }
    ins = {k: np.ascontiguousarray(v) for k, v in ins.items()}
    nc = bacc.Bacc("TRN2", target_bir_lowering=False, num_devices=1)
    aps = {k: nc.dram_tensor(k, v.shape, F32, kind="ExternalInput").ap() for k, v in ins.items()}
    out = nc.dram_tensor("out", (TILES, P, D), F32, kind="ExternalOutput").ap()
    fused_block(nc, out=out, **aps)
    got = run_bass_kernel_spmd(nc, [ins], core_ids=[0]).results[0]["out"]
    return got.reshape(T, B, D).transpose(1, 0, 2)
```

```python
from contextlib import ExitStack

import concourse.bass as bass
from concourse import mybir

F32 = mybir.dt.float32
U32 = mybir.dt.uint32
ALU = mybir.AluOpType
ACT = mybir.ActivationFunctionType
AX = mybir.AxisListType

P = 128
B = 32
D = 256
KD = D // P
H, DH = 16, 16
PATCHES, TXT = 36, 32
T = PATCHES + TXT
STEPS = P // B
TILES = T // STEPS
PATCH_TILES = PATCHES // STEPS
PD = 768
KP = PD // P
HG = 4
GH = H // HG
GW = GH * DH
GC = 3 * GW + 2 * GH
E = 8
F = 256
EPS_LN = 1e-5
EPS_N2 = 1e-24
BANK = 512
XIN = 3
PROJECTED = {-2: [1, 2], -1: [3, 4], 0: [5, 6], 1: [8]}
PROJECTED_FIRST = {1: [7]}
MOVES = 16 * 4
assert STEPS == HG == 4


def fused_block(nc, patches, txt, w_patch, patch_bias, w_qkvg, gate_bias, w_out, w_router, w_up, w_down,
                w_shared_up, w_shared_down, selector, identity, out):
    with ExitStack() as ctx:
        def sb(name, shape, dt=F32):
            return ctx.enter_context(nc.sbuf_tensor(name, shape, dt))

        def sem(name):
            return ctx.enter_context(nc.semaphore(name))

        wp = sb("wp", [P, KP, D])
        pbias = sb("pbias", [STEPS + 1, PATCH_TILES, D])
        sel = sb("sel", [STEPS + 1, P])
        wq = sb("wq", [P, KD, HG * GC])
        gbias = sb("gbias", [P, 2 * GH])
        wo = sb("wo", [P, KD, D])
        wr = sb("wr", [P, KD, E + 1])
        wu = sb("wu", [P, E, KD, F])
        wd = sb("wd", [P, E, KD, D])
        wsu = sb("wsu", [P, KD, 2 * F])
        wsd = sb("wsd", [P, KD, D])
        ident = sb("ident", [P, P])
        minus_half = sb("minus_half", [P, 2 * GH * STEPS])
        iota8 = sb("iota8", [P, E])

        xin = sb("xin", [P, XIN, KP, P])
        h_all = sb("h_all", [P, TILES, D])
        xn = sb("xn", [P, D])
        xT = sb("xT", [P, KD, P])
        qkvg = sb("qkvg", [P, HG * GC])
        rin = sb("rin", [P, 2, STEPS, GC])
        sq = sb("sq", [P, STEPS, 2 * GW])
        n2 = sb("n2", [P, STEPS, 2, GH])
        n2c = sb("n2c", [P, STEPS, 2, GH])
        inv = sb("inv", [P, STEPS, 2, GH])
        gz = sb("gz", [P, STEPS, 2 * GH])
        gt = sb("gt", [P, STEPS, 2 * GH])
        gates = sb("gates", [P, 2, STEPS, 2, GH])
        ia = sb("ia", [P, 2, STEPS, 2, GH])
        iab = sb("iab", [P, STEPS, GH])
        kk = sb("kk", [P, 2, 2, STEPS, GH, DH])
        vb = sb("vb", [P, 2, STEPS, GW])
        pq = sb("pq", [P, STEPS, GH, DH])
        kqr = sb("kqr", [P, STEPS, GH])
        kq = sb("kq", [P, 2, STEPS, GH])
        S = sb("S", [P, 2, GH, DH, DH])
        prod = sb("prod", [P, GH, DH, DH])
        rsum = sb("rsum", [P, GW])
        ub = sb("ub", [P, STEPS, GW])
        outer = sb("outer", [P, GH, DH, DH])
        qprod = sb("qprod", [P, GH, DH, DH])
        folded = sb("folded", [P, 2, 2, GH * DH, DH // 2])
        o1 = sb("o1", [P, STEPS, GW])
        o2 = sb("o2", [P, STEPS, GW])
        og = sb("og", [P, STEPS, GW])
        otok = sb("otok", [P, D])
        oT = sb("oT", [P, KD, P])
        h1 = sb("h1", [P, 2, D])
        x2n = sb("x2n", [P, D])
        x2T = sb("x2T", [P, 2, KD, P])
        stat = sb("stat", [P, 2, 6])
        mv = sb("mv", [P, 2, 2])
        veps = sb("veps", [P, 2, 1])
        mneg = sb("mneg", [P, 2, 1])
        rstd = sb("rstd", [P, 2, 1])
        shift = sb("shift", [P, 2, 1])
        carrier = sb("carrier", [P, 1])
        carried = sb("carried", [P, 1])
        lg = sb("lg", [P, E + 1])
        top8 = sb("top8", [P, 8])
        topi = sb("topi", [P, 8], U32)
        topf = sb("topf", [P, 8])
        z9 = sb("z9", [P, E + 1])
        t9 = sb("t9", [P, E + 1])
        num = sb("num", [P, E])
        den = sb("den", [P, E])
        rden = sb("rden", [P, E])
        ex = sb("ex", [P, E])
        esum = sb("esum", [P, 1])
        rsm = sb("rsm", [P, 1])
        mask1 = sb("mask1", [P, E])
        mask2 = sb("mask2", [P, E])
        comb = sb("comb", [P, 2, E + 1])
        hs = sb("hs", [P, 4, 2, KD, P])
        sg = sb("sg", [P, KD, P])
        hsh = sb("hsh", [P, KD, P])
        scaled = sb("scaled", [P, 2, 2, D])
        yfold = sb("yfold", [P, 2, D])
        ysum = sb("ysum", [P, D])
        acc = sb("acc", [P, 2, D])

        qkvg_dram = nc.dram_tensor("qkvg_dram", [2, P, HG * GC], F32).ap()
        o_dram = nc.dram_tensor("o_dram", [2, P, STEPS * GW], F32).ap()

        bank = [ctx.enter_context(nc.psum_tensor(f"bank{i}", [P, BANK], F32)) for i in range(5)]
        oq = ctx.enter_context(nc.psum_tensor("oq", [P, STEPS, GH * DH], F32))
        decayed = ctx.enter_context(nc.psum_tensor("decayed", [P, GH, DH, DH], F32))

        ld_patch, ld_attn, ld_out, ld_txt, ld_router, ld_up, ld_down, ld_shared = (
            sem(n) for n in ("ld_patch", "ld_attn", "ld_out", "ld_txt", "ld_router", "ld_up", "ld_down", "ld_shared"))
        rin_in, otok_in, acc_free, qkvg_out, o_out = (
            [sem(f"{n}{k}") for k in range(2)]
            for n in ("rin_in", "otok_in", "acc_free", "qkvg_out", "o_out"))
        xin_in = [sem(f"xin_in{k}") for k in range(XIN)]
        const_ready = sem("const_ready")
        pe_h, pe_xT, pe_qkv, pe_oT, pe_wout, pe_x2T, pe_router, pe_up, pe_gu, pe_down, pe_oq = (
            sem(n) for n in ("pe_h", "pe_xT", "pe_qkv", "pe_oT", "pe_wout", "pe_x2T", "pe_router", "pe_up", "pe_gu",
                             "pe_down", "pe_oq"))
        (act_h, act_xT, act_qkv, act_oT, act_x2T, act_hs, act_sg, act_sq, act_gt, act_t9, act_decay, act_xn,
         act_x2n, act_scaled) = (
            sem(n) for n in ("act_h", "act_xT", "act_qkv", "act_oT", "act_x2T", "act_hs", "act_sg", "act_sq",
                             "act_gt", "act_t9", "act_decay", "act_xn", "act_x2n", "act_scaled"))
        pool_rstd1, pool_rstd2, pool_inv, pool_qprod, pool_folded, pool_prep, pool_o2, pool_ysum = (
            sem(n) for n in ("pool_rstd1", "pool_rstd2", "pool_inv", "pool_qprod", "pool_folded", "pool_prep",
                             "pool_o2", "pool_ysum"))
        (dve_st1, dve_st2, dve_h1, dve_gz, dve_n2, dve_n2c, dve_gates, dve_kqr, dve_kq, dve_prod, dve_rsum,
         dve_u, dve_outer, dve_state, dve_o1, dve_o, dve_logits, dve_z9, dve_route, dve_comb, dve_acc,
         dve_gu, dve_gsum) = (
            sem(n) for n in ("dve_st1", "dve_st2", "dve_h1", "dve_gz", "dve_n2", "dve_n2c", "dve_gates", "dve_kqr",
                             "dve_kq", "dve_prod", "dve_rsum", "dve_u", "dve_outer", "dve_state", "dve_o1", "dve_o",
                             "dve_logits", "dve_z9", "dve_route", "dve_comb", "dve_acc", "dve_gu", "dve_gsum"))

        block = ctx.enter_context(nc.Block())

        def stages(i):
            return {"A": 0 <= i + 2 < TILES, "B": 0 <= i + 1 < TILES,
                    "R": 0 <= i < TILES, "O": 0 <= i - 1 < TILES, "M": 0 <= i - 2 < TILES}

        FIRST, LAST = -2, TILES + 1

        def is_at(i, n):
            return isinstance(i, int) and i == n

        def is_from(i, n):
            return not isinstance(i, int) or i >= n

        def projected(i, tiles):
            return tiles.get(i, []) if isinstance(i, int) else []

        def run(eng, body):
            def peeled(first, last):
                for i in range(first, last):
                    body(i, i % 2, stages(i), lambda off: (i + off) // 2)

            def pairs(first, last):
                with eng.Fori(0, (last - first) // 2) as pair:
                    for n in range(2):
                        c = first + n
                        body(pair * 2 + c, c % 2, stages(c), lambda off: pair + (c + off) // 2)

            peeled(FIRST, 3)
            pairs(3, TILES - 2)
            peeled(TILES - 2, LAST + 1)

        bank_order = [
            [("router", "M", -2, dve_logits, 1, 1), ("xT", "A", 2, act_xT, 1, 1),
             ("oT", "O", -1, act_oT, 1, 1), ("qkv0", "A", 2, act_qkv, 2, 1), ("gu", "M", -2, dve_gu, 1, 1)],
            [("up2", "M", -2, act_hs, 4, 3), ("up3", "M", -2, act_hs, 4, 4), ("down2", "M", -2, act_scaled, 4, 4),
             ("downS", "M", -2, dve_acc, 4, 4)],
            [("up0", "M", -2, act_hs, 4, 1), ("wout", "O", -1, dve_h1, 1, 1), ("qkv1", "A", 2, act_qkv, 2, 2)],
            [("up1", "M", -2, act_hs, 4, 2), ("down1", "M", -2, act_scaled, 4, 2), ("x2T", "O", -1, act_x2T, 1, 1)],
            [("down0", "M", -2, dve_acc, 4, 1), ("down3", "M", -2, dve_acc, 4, 3)],
        ]
        h_banks = [bank[1], bank[4]]
        bank_of = {group[0]: n for n, order in enumerate(bank_order) for group in order}

        def take(pe, name, i, st, before):
            for b, order in enumerate(bank_order):
                names = [g[0] for g in order]
                if name in names:
                    at = names.index(name)
                    back = [(g, 0, st) for g in reversed(order[:at])] + [(g, -1, before) for g in reversed(order)]
                    for (_, stage, off, s, per, nth), turn, live in back:
                        if live[stage]:
                            pe.wait_ge(s, (i + (off + turn)) * per + nth)
                            break
                    return bank[b]

        @block.sync
        def _(sp):
            sp.dma_start(sel[:], selector).then_inc(ld_patch, 16)
            sp.dma_start(pbias[:], patch_bias).then_inc(ld_patch, 16)
            sp.dma_start(xin[:, 0], patches[0]).then_inc(xin_in[0], 16)
            sp.dma_start(wp[:], w_patch).then_inc(ld_patch, 16)
            sp.dma_start(ident[:], identity).then_inc(ld_attn, 16)
            sp.dma_start(wq[:], w_qkvg).then_inc(ld_attn, 16)
            sp.dma_start(gbias[:], gate_bias).then_inc(ld_attn, 16)
            for tile in range(1, XIN):
                sp.dma_start(xin[:, tile], patches[tile]).then_inc(xin_in[tile], 16)

            def body(i, par, st, half):
                if st["O"]:
                    sp.wait_ge(dve_o, i)
                    sp.dma_start(o_dram[1 - par], og[:]).then_inc(o_out[1 - par], 16)
                    sp.wait_ge(o_out[1 - par], (half(-1) + 1) * 16)
                    for s in range(STEPS):
                        sp.dma_start(otok[s * B:(s + 1) * B],
                                     o_dram[1 - par, :, s * GW:(s + 1) * GW].rearrange("(g b) c -> b g c", g=HG))\
                          .then_inc(otok_in[1 - par], 16)
                if is_at(i, 1):
                    sp.dma_start(wsu[:], w_shared_up).then_inc(ld_shared, 16)
                    sp.dma_start(wsd[:], w_shared_down).then_inc(ld_shared, 16)
                    sp.dma_start(h_all[:, PATCH_TILES:TILES], txt).then_inc(ld_txt, 16)
                if st["A"]:
                    sp.wait_ge(act_qkv, (i + 3) * 2)
                    sp.dma_start(qkvg_dram[par], qkvg[:]).then_inc(qkvg_out[par], 16)
                    if is_from(i, 0):
                        sp.wait_ge(pool_qprod, (i + 1) * STEPS)
                    sp.wait_ge(qkvg_out[par], (half(2) + 1) * 16)
                    for g in range(HG):
                        sp.dma_start(rin[g * B:(g + 1) * B, par],
                                     qkvg_dram[par, :, g * GC:(g + 1) * GC].rearrange("(s b) c -> b s c", s=STEPS))\
                          .then_inc(rin_in[par], 16)
                for tile in projected(i, PROJECTED):
                    if tile + XIN - 1 < PATCH_TILES:
                        sp.wait_ge(pe_h, tile)
                        sp.dma_start(xin[:, (tile - 1) % XIN], patches[tile + XIN - 1])\
                          .then_inc(xin_in[(tile - 1) % XIN], 16)
                if is_at(i, -2):
                    sp.dma_start(wo[:], w_out).then_inc(ld_out, 16)
                    sp.dma_start(wr[:], w_router).then_inc(ld_router, 16)
                if is_at(i, -1):
                    sp.dma_start(wu[:], w_up).then_inc(ld_up, 16)
                    sp.dma_start(wd[:], w_down).then_inc(ld_down, 16)
                if st["M"]:
                    sp.wait_ge(dve_acc, (i - 1) * 4)
                    sp.dma_start(out[i - 2], acc[:, par]).then_inc(acc_free[par], 16)

            run(sp, body)
            for k in range(2):
                sp.wait_ge(acc_free[k], 16 + 16 * ((TILES + 1 - k) // 2))

        @block.tensor
        def _(pe):
            def matmuls(dst, pairs, done=None):
                for n, (l, r) in enumerate(pairs):
                    mm = pe.matmul(dst, l, r, start=(n == 0), stop=(n == len(pairs) - 1))
                if done is not None:
                    mm.then_inc(done, 1)

            def project(tile):
                if tile >= 2:
                    pe.wait_ge(act_h, tile - 1)
                pe.wait_ge(xin_in[tile % XIN], (tile // XIN + 1) * 16)
                dst = h_banks[tile % 2][:, 0:D]
                pe.matmul(dst, sel[:], pbias[:, tile, :], start=True, stop=False)
                for d in range(KP):
                    mm = pe.matmul(dst, xin[:, tile % XIN, d, :], wp[:, d, :], start=False, stop=(d == KP - 1))
                mm.then_inc(pe_h, 1)

            pe.wait_ge(ld_patch, 48)
            project(0)
            project(1)

            def body(i, par, st, half):
                before = stages(i - 1) if isinstance(i, int) else st
                first = is_at(i, FIRST)

                def up(k):
                    dst = take(pe, f"up{k}", i, st, before)
                    if is_at(i, 2):
                        pe.wait_ge(ld_up, 16)
                    for e in range(2):
                        for f in range(KD):
                            c = (e * KD + f) * P
                            matmuls(dst[:, c:c + P],
                                    [(wu[:, 2 * k + e, d, f * P:(f + 1) * P], x2T[:, par, d, :]) for d in range(KD)],
                                    pe_up if (e, f) == (1, KD - 1) else None)

                def down(k):
                    dst = take(pe, f"down{k}", i, st, before)
                    if is_at(i, 2):
                        pe.wait_ge(ld_down, 16)
                    pe.wait_ge(act_hs, (i - 2) * 4 + k + 1)
                    for e in range(2):
                        matmuls(dst[:, e * D:(e + 1) * D],
                                [(hs[:, k, e, f, :], wd[:, 2 * k + e, f, :]) for f in range(KD)],
                                pe_down if e else None)

                def turned(name, s, src):
                    dst = take(pe, name, i, st, before)
                    for d in range(KD):
                        tr = pe.transpose(dst[:, d * P:(d + 1) * P], src[:, d * P:(d + 1) * P], ident[:])
                    tr.then_inc(s, 1)

                def read_out(tile, pair):
                    pe.wait_ge(pool_folded, tile * STEPS + 2 * pair + 2)
                    if pair == 0 and (is_from(i, 1)):
                        pe.wait_ge(dve_o1, tile)
                    matmuls(oq[:, 2 * pair:2 * pair + 2, :].rearrange("p s c -> p (s c)"),
                            [(ident[:], folded[:, pair].rearrange("p s c j -> p (s c) j")[:, :, j])
                             for j in range(DH // 2)], pe_oq)

                if st["M"]:
                    if is_at(i, 2):
                        pe.wait_ge(act_h, PATCH_TILES)
                    dst = take(pe, "router", i, st, before)
                    if is_at(i, 2):
                        pe.wait_ge(ld_router, 16)
                    pe.wait_ge(act_x2T, i - 1)
                    matmuls(dst[:, 0:E + 1], [(x2T[:, par, d, :], wr[:, d, :]) for d in range(KD)], pe_router)
                early = isinstance(i, int) and i <= 2
                if st["O"] and early:
                    read_out(i - 1, 1)
                for tile in projected(i, PROJECTED_FIRST):
                    project(tile)
                if st["M"]:
                    up(0)
                    up(1)
                if st["O"] and not early:
                    read_out(i - 1, 1)
                if st["M"]:
                    down(0)
                    up(2)
                    down(1)
                    up(3)
                if st["A"]:
                    if first:
                        pe.wait_ge(ld_attn, 48)
                    pe.wait_ge(act_xn, i + 3)
                    turned("xT", pe_xT, xn)
                if st["O"]:
                    pe.wait_ge(otok_in[1 - par], (half(-1) + 1) * MOVES)
                    turned("oT", pe_oT, otok)
                    dst = take(pe, "wout", i, st, before)
                    pe.wait_ge(act_oT, i)
                    if is_at(i, 1):
                        pe.wait_ge(ld_out, 16)
                    matmuls(dst[:, 0:D], [(oT[:, d, :], wo[:, d, :]) for d in range(KD)], pe_wout)
                if st["A"]:
                    pe.wait_ge(act_xT, i + 3)
                    cols = HG * GC // 2
                    for n in range(2):
                        dst = take(pe, f"qkv{n}", i, st, before)
                        matmuls(dst[:, 0:cols], [(xT[:, d, :], wq[:, d, n * cols:(n + 1) * cols]) for d in range(KD)],
                                pe_qkv)
                if st["M"]:
                    down(2)
                if st["R"]:
                    read_out(i, 0)
                if st["M"]:
                    dst = take(pe, "gu", i, st, before)
                    if is_at(i, 2):
                        pe.wait_ge(ld_shared, 32)
                    for f in range(2 * KD):
                        matmuls(dst[:, f * P:(f + 1) * P],
                                [(wsu[:, d, f * P:(f + 1) * P], x2T[:, par, d, :]) for d in range(KD)],
                                pe_gu if f == 2 * KD - 1 else None)
                    down(3)
                if st["O"]:
                    pe.wait_ge(act_x2n, i)
                    turned("x2T", pe_x2T, x2n)
                if st["M"]:
                    dst = take(pe, "downS", i, st, before)
                    pe.wait_ge(dve_gu, i - 1)
                    matmuls(dst[:, 0:D], [(hsh[:, f, :], wsd[:, f, :]) for f in range(KD)], pe_down)
                for tile in projected(i, PROJECTED):
                    if tile > 1:
                        project(tile)

            run(pe, body)

        @block.scalar
        def _(act):
            act.preload_act_table_set("silu_and_others")

            def project(tile):
                act.wait_ge(pe_h, tile + 1)
                act.activation(h_all[:, tile, :], h_banks[tile % 2][:, 0:D], ACT.Copy).then_inc(act_h, 1)

            project(0)

            def body(i, par, st, half):
                def decay(s):
                    act.wait_ge(dve_state, i * STEPS + s + 1)
                    if s == 0:
                        act.wait_ge(dve_gates, i + 1)
                    for g in range(GH):
                        act.activation(decayed[:, g], S[:, (s + 1) % 2, g], ACT.Copy,
                                       scale=gates[:, par, s, 0, g:g + 1]).then_inc(act_decay, 1)

                def hidden(k):
                    act.wait_ge(pe_up, (i - 2) * 4 + k + 1)
                    if is_from(i, 3):
                        act.wait_ge(pe_down, (i - 3) * 5 + k + 1)
                    act.activation(hs[:, k].rearrange("p e f t -> p (e f t)"), bank[bank_of[f"up{k}"]][:], ACT.Silu)\
                       .then_inc(act_hs, 1)

                def evacuate(name, dst, waited, count, done):
                    act.wait_ge(waited, count)
                    act.activation(dst, bank[bank_of[name]][:, 0:D], ACT.Copy).then_inc(done, 1)

                def weighted(k):
                    act.wait_ge(pe_down, (i - 2) * 5 + k + 1)
                    if k == 1:
                        act.wait_ge(dve_comb, i - 1)
                        if is_from(i, 3):
                            act.wait_ge(pool_ysum, (i - 2) * 2)
                    for e in range(2):
                        act.activation(scaled[:, k - 1, e], bank[bank_of[f"down{k}"]][:, e * D:(e + 1) * D], ACT.Copy,
                                       scale=comb[:, par, 2 * k + e:2 * k + e + 1]).then_inc(act_scaled, 1)

                def normalised(which, dst, src, ready, count, done):
                    act.wait_ge(ready, count)
                    if which == 0:
                        act.activation(carried[:], shift[:, 0], ACT.Copy)
                    act.activation(dst, src, ACT.Identity, bias=shift[:, which], scale=rstd[:, which]).then_inc(done, 1)

                first_experts = is_at(i, 2)
                if st["M"] and not first_experts:
                    hidden(0)
                    hidden(1)
                if st["R"]:
                    decay(0)
                if st["B"]:
                    act.wait_ge(rin_in[1 - par], (half(1) + 1) * MOVES)
                    if is_from(i, 0):
                        act.wait_ge(dve_n2, i + 1)
                    act.activation(sq[:], rin[:, 1 - par, :, 0:2 * GW], ACT.Square).then_inc(act_sq, 1)
                if first_experts:
                    hidden(0)
                    hidden(1)
                if st["M"]:
                    act.wait_ge(dve_z9, (i - 1) * 2)
                    act.activation(t9[:], z9[:], ACT.Tanh, scale=0.5).then_inc(act_t9, 1)
                    hidden(2)
                if st["A"]:
                    if is_from(i, FIRST + 1):
                        act.wait_ge(pe_xT, i + 2)
                    normalised(0, xn[:], h_all[:, i + 2, :], pool_rstd1, (i + 3) * 2, act_xn)
                for tile in projected(i, PROJECTED_FIRST):
                    project(tile)
                if st["R"]:
                    decay(1)
                if st["A"]:
                    evacuate("xT", xT[:].rearrange("p d t -> p (d t)"), pe_xT, i + 3, act_xT)
                if st["O"]:
                    evacuate("oT", oT[:].rearrange("p d t -> p (d t)"), pe_oT, i, act_oT)
                if st["M"]:
                    weighted(1)
                if st["B"]:
                    act.wait_ge(dve_gz, i + 2)
                    act.activation(gt[:], gz[:], ACT.Tanh, scale=0.5).then_inc(act_gt, 1)
                if st["M"]:
                    hidden(3)
                if st["R"]:
                    decay(2)
                if st["A"]:
                    cols = HG * GC // 2
                    for n in range(2):
                        act.wait_ge(pe_qkv, (i + 2) * 2 + n + 1)
                        if n == 0 and (is_from(i, FIRST + 1)):
                            act.wait_ge(qkvg_out[1 - par], (half(1) + 1) * 16)
                        act.activation(qkvg[:, n * cols:(n + 1) * cols], bank[bank_of[f"qkv{n}"]][:, 0:cols],
                                       ACT.Copy).then_inc(act_qkv, 1)
                if st["M"]:
                    weighted(2)
                    act.wait_ge(pe_gu, i - 1)
                    if is_from(i, 3):
                        act.wait_ge(dve_gu, i - 2)
                    act.activation(sg[:].rearrange("p f t -> p (f t)"), bank[bank_of["gu"]][:, 0:F], ACT.Silu)\
                       .then_inc(act_sg, 1)
                if st["O"]:
                    if is_from(i, 2):
                        act.wait_ge(pe_x2T, i - 1)
                    normalised(1, x2n[:], h1[:, 1 - par], pool_rstd2, i * 2, act_x2n)
                if st["R"]:
                    decay(3)
                if st["O"]:
                    evacuate("x2T", x2T[:, 1 - par].rearrange("p d t -> p (d t)"), pe_x2T, i, act_x2T)
                for tile in projected(i, PROJECTED):
                    project(tile)

            run(act, body)

        @block.gpsimd
        def _(pool):
            PREP = 6
            pool.memset(minus_half[:], -0.5).then_inc(const_ready, 1)
            pool.iota(topi[:], pattern=[[1, 8]], base=0, channel_multiplier=0).then_inc(const_ready, 1)
            pool.wait_ge(const_ready, 2)
            pool.tensor_copy(iota8[:], topi[:]).then_inc(const_ready, 1)
            pool.wait_ge(const_ready, 3)

            def body(i, par, st, half):
                def read_out(s):
                    at = i * STEPS + s
                    pool.wait_ge(dve_state, at + 1)
                    if not isinstance(i, int) or at >= 1:
                        pool.wait_ge(pool_folded, at)
                    q = rin[:, par, s, 0:GW].rearrange("p (h d) -> p h d", h=GH)
                    pool.tensor_tensor(qprod[:], S[:, (s + 1) % 2], q.unsqueeze(2).to_broadcast([P, GH, DH, DH]),
                                       ALU.mult).then_inc(pool_qprod, 1)
                    qrows = qprod[:].rearrange("p h r d -> p (h r) d")
                    pool.wait_ge(pool_qprod, at + 1)
                    if is_from(i, 1):
                        pool.wait_ge(pe_oq, i * 2 - 1 + s // 2)
                    pool.tensor_tensor(folded[:, s // 2, s % 2], qrows[:, :, 0:DH // 2], qrows[:, :, DH // 2:DH],
                                       ALU.add).then_inc(pool_folded, 1)

                def deviation(which, s, tile, stats):
                    pool.wait_ge(stats, (tile + 1) * 4)
                    if not isinstance(i, int) or tile >= 1:
                        pool.wait_ge((act_xn, act_x2n)[which], tile)
                    pool.tensor_tensor(rstd[:, which], veps[:, which], minus_half[:, 0:1], ALU.pow).then_inc(s, 1)
                    pool.wait_ge(s, tile * 2 + 1)
                    pool.tensor_tensor(shift[:, which], mneg[:, which], rstd[:, which], ALU.mult).then_inc(s, 1)

                def heads(ap):
                    return ap.rearrange("p s (h d) -> p s h d", h=GH)

                def over_width(ap):
                    return ap.unsqueeze(3).to_broadcast([P, STEPS, GH, DH])

                def norms():
                    pool.wait_ge(dve_n2c, i + 2)
                    if is_from(i, 0):
                        pool.wait_ge(dve_kq, i + 1)
                    pool.tensor_tensor(inv[:].rearrange("p s k h -> p (s k h)"),
                                       n2c[:].rearrange("p s k h -> p (s k h)"), minus_half[:],
                                       ALU.pow).then_inc(pool_inv, 1)

                def prepare():
                    q, k, v = (heads(rin[:, 1 - par, :, n * GW:(n + 1) * GW]) for n in range(3))
                    alpha, beta = (gates[:, 1 - par, :, n, :] for n in range(2))
                    at = (i + 1) * PREP
                    pool.wait_ge(pool_inv, i + 2)
                    pool.tensor_tensor(kk[:, 1 - par, 0], k, over_width(inv[:, :, 1, :]), ALU.mult)\
                        .then_inc(pool_prep, 1)
                    pool.wait_ge(dve_gates, i + 2)
                    if is_from(i, 1):
                        pool.wait_ge(dve_o1, i)
                    pool.tensor_tensor(ia[:, 1 - par], inv[:], alpha.unsqueeze(2).to_broadcast([P, STEPS, 2, GH]),
                                       ALU.mult).then_inc(pool_prep, 1)
                    pool.tensor_tensor(heads(vb[:, 1 - par]), v, over_width(beta), ALU.mult).then_inc(pool_prep, 1)
                    pool.wait_ge(pool_prep, at + 2)
                    pool.tensor_tensor(iab[:], ia[:, 1 - par, :, 1, :], beta, ALU.mult).then_inc(pool_prep, 1)
                    pool.tensor_tensor(pq[:], kk[:, 1 - par, 0], q, ALU.mult).then_inc(pool_prep, 1)
                    pool.wait_ge(pool_prep, at + 4)
                    pool.tensor_tensor(kk[:, 1 - par, 1], k, over_width(iab[:]), ALU.mult).then_inc(pool_prep, 1)

                if st["R"]:
                    read_out(0)
                if st["A"]:
                    deviation(0, pool_rstd1, i + 2, dve_st1)
                if st["B"]:
                    norms()
                if st["R"]:
                    read_out(1)
                    read_out(2)
                if st["O"]:
                    deviation(1, pool_rstd2, i - 1, dve_st2)
                if st["M"]:
                    pool.wait_ge(act_scaled, (i - 1) * 4)
                    pool.tensor_tensor(yfold[:], scaled[:, 0], scaled[:, 1], ALU.add).then_inc(pool_ysum, 1)
                    pool.wait_ge(pool_ysum, (i - 2) * 2 + 1)
                    if is_from(i, 3):
                        pool.wait_ge(dve_acc, (i - 2) * 4 - 2)
                    pool.tensor_tensor(ysum[:], yfold[:, 0], yfold[:, 1], ALU.add).then_inc(pool_ysum, 1)
                if st["B"]:
                    prepare()
                if st["R"]:
                    read_out(3)
                    pool.wait_ge(dve_u, (i + 1) * STEPS)
                    pool.wait_ge(dve_kq, i + 1)
                    if is_from(i, 1):
                        pool.wait_ge(dve_o, i)
                    pool.tensor_tensor(heads(o2[:]), heads(ub[:]), over_width(kq[:, par]), ALU.mult)\
                        .then_inc(pool_o2, 1)

            run(pool, body)

        @block.vector
        def _(dve):
            PREP, ROUTE = 6, 12
            dve.memset(S[:, 1], 0.0).then_inc(dve_state, 1)
            for k in range(2):
                dve.memset(acc[:, k], 0.0).then_inc(acc_free[k], 16)
            dve.wait_ge(const_ready, 3)

            def body(i, par, st, half):
                inner = not isinstance(i, int)

                def moments(which, src, s):
                    dve.bn_stats(stat[:, which], src).then_inc(s, 1)

                def mean_and_variance(which, s, tile, used):
                    dve.wait_ge(s, tile * 4 + 1)
                    if inner or tile >= 1:
                        dve.wait_ge(used, tile * 2)
                    dve.memset(carrier[:], 0.0)
                    dve.bn_aggr(mv[:, which], stat[:, which]).then_inc(s, 1)

                def variance_plus_epsilon(which, s, tile):
                    dve.wait_ge(s, tile * 4 + 2)
                    dve.tensor_scalar(veps[:, which], mv[:, which, 1:2], EPS_LN, None, ALU.add).then_inc(s, 1)
                    dve.tensor_scalar(mneg[:, which], mv[:, which, 0:1], -1.0, None, ALU.mult).then_inc(s, 1)

                def residual():
                    dve.wait_ge(pe_wout, i)
                    dve.tensor_tensor(h1[:, 1 - par], bank[bank_of["wout"]][:, 0:D], h_all[:, i - 1, :], ALU.add)\
                       .then_inc(dve_h1, 1)

                def norm_1_moments():
                    if not inner and i <= 2:
                        dve.wait_ge(act_h, i + 3)
                    moments(0, h_all[:, i + 2, :], dve_st1)

                def norm_1_mean():
                    mean_and_variance(0, dve_st1, i + 2, pool_rstd1)

                def norm_1_epsilon():
                    variance_plus_epsilon(0, dve_st1, i + 2)

                def norm_2_moments():
                    dve.wait_ge(dve_h1, i)
                    moments(1, h1[:, 1 - par], dve_st2)

                def norm_2_mean():
                    mean_and_variance(1, dve_st2, i - 1, pool_rstd2)

                def norm_2_epsilon():
                    variance_plus_epsilon(1, dve_st2, i - 1)

                def add_expert(n):
                    k, first = n // 2, n in (0, 6)
                    if n == 0:
                        dve.wait_ge(pe_down, (i - 2) * 5 + 1)
                        dve.wait_ge(dve_comb, i - 1)
                        dve.wait_ge(acc_free[par], (half(-2) + 1) * 16)
                    elif first or n == E:
                        dve.wait_ge(pe_down, (i - 2) * 5 + k + 1)
                        dve.wait_ge(dve_acc, (i - 2) * 4 + k - 1)
                    else:
                        dve.wait_ge(dve_gsum, (i - 2) * 2 + (1 if k == 0 else 2))
                    product = bank[bank_of[f"down{k}" if n < E else "downS"]][:, n % 2 * D:(n % 2 + 1) * D]
                    dve.scalar_tensor_tensor(acc[:, par], product,
                                             comb[:, par, n:n + 1], h1[:, par] if n == 0 else acc[:, par],
                                             ALU.mult, ALU.add).then_inc(dve_gsum if first else dve_acc, 1)

                def add_weighted():
                    dve.wait_ge(pool_ysum, (i - 1) * 2)
                    dve.wait_ge(dve_acc, (i - 2) * 4 + 1)
                    dve.tensor_tensor(acc[:, par], acc[:, par], ysum[:], ALU.add).then_inc(dve_acc, 1)

                def gated_up():
                    dve.wait_ge(act_sg, i - 1)
                    if inner or i >= 3:
                        dve.wait_ge(pe_down, (i - 2) * 5)
                    dve.tensor_tensor(hsh[:].rearrange("p f t -> p (f t)"), bank[bank_of["gu"]][:, F:2 * F],
                                      sg[:].rearrange("p f t -> p (f t)"), ALU.mult).then_inc(dve_gu, 1)

                def gate_inputs():
                    dve.wait_ge(rin_in[1 - par], (half(1) + 1) * MOVES)
                    if not inner and i == -1:
                        dve.wait_ge(ld_attn, 48)
                    dve.tensor_tensor(gz[:], rin[:, 1 - par, :, 3 * GW:GC],
                                      gbias[:].unsqueeze(1).to_broadcast([P, STEPS, 2 * GH]), ALU.add)\
                       .then_inc(dve_gz, 1)

                def norms_squared():
                    dve.wait_ge(act_sq, i + 2)
                    dve.tensor_reduce(n2[:].rearrange("p s k h -> p s (k h)"),
                                      sq[:].rearrange("p s (m d) -> p s m d", d=DH), AX.X, ALU.add).then_inc(dve_n2, 1)

                def norms_guarded():
                    dve.wait_ge(dve_n2, i + 2)
                    dve.tensor_scalar(n2c[:], n2[:], EPS_N2, None, ALU.max).then_inc(dve_n2c, 1)

                def gate_values():
                    dve.wait_ge(act_gt, i + 2)
                    dve.tensor_scalar(gates[:, 1 - par].rearrange("p s k h -> p s (k h)"), gt[:], 0.5, 0.5, ALU.mult,
                                      ALU.add).then_inc(dve_gates, 1)

                def kq_sum():
                    dve.wait_ge(pool_prep, (i + 1) * PREP + 5)
                    dve.tensor_reduce(kqr[:], pq[:], AX.X, ALU.add).then_inc(dve_kqr, 1)

                def kq_scaled():
                    dve.wait_ge(dve_kqr, i + 2)
                    dve.tensor_tensor(kq[:, 1 - par], kqr[:], inv[:, :, 0, :], ALU.mult).then_inc(dve_kq, 1)

                def step(s, fill):
                    t = i * STEPS + s
                    old, new = S[:, (s + 1) % 2], S[:, s % 2]
                    shape = [P, GH, DH, DH]
                    dve.wait_ge(dve_state, t + 1)
                    if s == 0:
                        dve.wait_ge(pool_prep, (i + 1) * PREP)
                    dve.tensor_tensor(prod[:], old, kk[:, par, 1, s].unsqueeze(2).to_broadcast(shape), ALU.mult)\
                       .then_inc(dve_prod, 1)
                    fill()
                    dve.wait_ge(dve_prod, t + 1)
                    dve.tensor_reduce(rsum[:].rearrange("p (h r) -> p h r", h=GH), prod[:], AX.X, ALU.add)\
                       .then_inc(dve_rsum, 1)
                    fill()
                    dve.wait_ge(dve_rsum, t + 1)
                    if s == 0 and (inner or i >= 1):
                        dve.wait_ge(pool_o2, i)
                    dve.tensor_tensor(ub[:, s, :], vb[:, par, s, :], rsum[:], ALU.subtract).then_inc(dve_u, 1)
                    fill()
                    dve.wait_ge(dve_u, t + 1)
                    u = ub[:, s, :].rearrange("p (h r) -> p h r", h=GH)
                    dve.tensor_tensor(outer[:], u.unsqueeze(3).to_broadcast(shape),
                                      kk[:, par, 0, s].unsqueeze(2).to_broadcast(shape), ALU.mult)\
                       .then_inc(dve_outer, 1)
                    fill()
                    dve.wait_ge(dve_outer, t + 1)
                    dve.wait_ge(act_decay, (t + 1) * GH)
                    if inner or i >= 1 or s >= 1:
                        dve.wait_ge(pool_qprod, t)
                    dve.tensor_tensor(new, decayed[:], outer[:], ALU.add).then_inc(dve_state, 1)
                    fill()

                def head_states():
                    dve.wait_ge(pe_oq, i * 2)
                    dve.tensor_tensor(o1[:].rearrange("p s (h d) -> p s h d", h=GH),
                                      oq[:].rearrange("p s (h d) -> p s h d", h=GH),
                                      ia[:, 1 - par, :, 0, :].unsqueeze(3).to_broadcast([P, STEPS, GH, DH]), ALU.mult)\
                       .then_inc(dve_o1, 1)

                def head_outputs():
                    dve.wait_ge(dve_o1, i)
                    dve.wait_ge(pool_o2, i)
                    if inner or i >= 2:
                        dve.wait_ge(o_out[par], (half(-2) + 1) * 16)
                        dve.wait_ge(pe_oT, i - 1)
                    dve.tensor_tensor(og[:], o1[:], o2[:], ALU.add).then_inc(dve_o, 1)

                at = (i - 2) * ROUTE

                def logits():
                    dve.wait_ge(pe_router, i - 1)
                    dve.tensor_copy(lg[:], bank[bank_of["router"]][:, 0:E + 1]).then_inc(dve_logits, 1)

                def largest():
                    dve.wait_ge(dve_logits, i - 1)
                    dve.tensor_copy(z9[:, E:E + 1], lg[:, E:E + 1]).then_inc(dve_z9, 1)
                    dve.max(top8[:], lg[:, 0:E]).then_inc(dve_route, 1)

                def less_largest():
                    dve.wait_ge(dve_route, at + 1)
                    dve.tensor_scalar(z9[:, 0:E], lg[:, 0:E], top8[:, 0:1], None, ALU.subtract).then_inc(dve_z9, 1)

                def places():
                    dve.max_index(topi[:], top8[:], lg[:, 0:E]).then_inc(dve_route, 1)

                def places_float():
                    dve.wait_ge(dve_route, at + 2)
                    dve.tensor_copy(topf[:], topi[:]).then_inc(dve_route, 1)

                def first_chosen():
                    dve.wait_ge(dve_route, at + 3)
                    dve.tensor_scalar(mask1[:], iota8[:], topf[:, 0:1], None, ALU.is_equal).then_inc(dve_route, 1)

                def both_chosen():
                    dve.wait_ge(dve_route, at + 4)
                    dve.scalar_tensor_tensor(mask2[:], iota8[:], topf[:, 1:2], mask1[:], ALU.is_equal, ALU.add)\
                       .then_inc(dve_route, 1)

                def exp_parts():
                    dve.wait_ge(act_t9, i - 1)
                    dve.tensor_scalar(den[:], t9[:, 0:E], -1.0, 1.0, ALU.mult, ALU.add).then_inc(dve_route, 1)
                    dve.tensor_scalar(num[:], t9[:, 0:E], 1.0, None, ALU.add).then_inc(dve_route, 1)
                    dve.tensor_scalar(comb[:, par, E:E + 1], t9[:, E:E + 1], 0.5, 0.5, ALU.mult, ALU.add)\
                       .then_inc(dve_route, 1)

                def exp_denominator():
                    dve.wait_ge(dve_route, at + 8)
                    dve.reciprocal(rden[:], den[:]).then_inc(dve_route, 1)

                def exps():
                    dve.wait_ge(dve_route, at + 9)
                    dve.tensor_tensor(ex[:], num[:], rden[:], ALU.mult).then_inc(dve_route, 1)

                def exp_sum():
                    dve.wait_ge(dve_route, at + 10)
                    dve.tensor_reduce(esum[:], ex[:], AX.X, ALU.add).then_inc(dve_route, 1)

                def over_sum():
                    dve.wait_ge(dve_route, at + 11)
                    dve.reciprocal(rsm[:], esum[:]).then_inc(dve_route, 1)

                def weights():
                    dve.wait_ge(dve_route, at + 12)
                    dve.scalar_tensor_tensor(comb[:, par, 0:E], ex[:], rsm[:], mask2[:], ALU.mult, ALU.mult)\
                       .then_inc(dve_comb, 1)

                def expert(n):
                    return ("M", lambda: add_expert(n))

                plan = [
                    [[("A", norm_1_moments), ("M", logits), ("O", head_states), ("A", norm_1_mean), ("M", largest)],
                     [("M", less_largest), ("O", head_outputs), ("A", norm_1_epsilon), ("B", norms_squared),
                      ("M", places)],
                     [("B", norms_guarded), ("M", places_float)],
                     [("M", first_chosen), ("B", gate_inputs), ("M", both_chosen), ("M", exp_parts)],
                     [("M", exp_denominator)]],
                    [[("M", exps)],
                     [("M", exp_sum)],
                     [("M", over_sum)],
                     [("M", weights), ("O", residual), expert(0)],
                     [expert(1), ("O", norm_2_moments)]],
                    [[("O", norm_2_mean)],
                     [("O", norm_2_epsilon)],
                     [("B", gate_values)],
                     [],
                     []],
                    [[("M", gated_up)],
                     [("M", add_weighted)],
                     [],
                     [expert(6), ("B", kq_sum)],
                     [expert(7), ("B", kq_scaled), expert(8)]],
                ]
                for s in range(STEPS):
                    turn = iter(plan[s])

                    def fill():
                        for stage, part in next(turn):
                            if st[stage]:
                                part()
                    if st["R"]:
                        step(s, fill)
                    else:
                        for _ in plan[s]:
                            fill()
                if not inner and i == 2:
                    dve.wait_ge(act_h, PATCH_TILES)
                    dve.wait_ge(ld_txt, 16)

            run(dve, body)


def kernel(x, txt, L0_tok_W, L0_tok_b, L0_tok_pos_embd, L0_attn_Wqkv, L0_attn_Wg, L0_attn_bg, L0_attn_Wb, L0_attn_bb,
           L0_attn_Wout, L0_ffn_router_w, L0_ffn_w1, L0_ffn_w2, L0_ffn_shared_gate_up, L0_ffn_shared_down,
           L0_ffn_shared_gate_w):
    import numpy as np
    import concourse.bacc as bacc
    from concourse.bass_utils import run_bass_kernel_spmd

    def a(v):
        return np.asarray(v)

    def blocked(w):
        return a(w).reshape(-1, P, w.shape[-1]).transpose(1, 0, 2)

    side = int(PATCHES ** 0.5)
    px = x.shape[-1] // side
    patches = a(x).reshape(B, 3, side, px, side, px).transpose(2, 4, 1, 3, 5, 0)
    patches = patches.reshape(PATCH_TILES, STEPS, KP, P, B).transpose(0, 3, 2, 1, 4)
    text = a(txt).transpose(1, 0, 2).reshape(TILES - PATCH_TILES, P, D).transpose(1, 0, 2)
    pos = a(L0_tok_pos_embd).reshape(PATCH_TILES, STEPS, D).transpose(1, 0, 2)
    bias = np.broadcast_to(a(L0_tok_b), (1, PATCH_TILES, D))
    qkv = a(L0_attn_Wqkv).reshape(3, HG, GW, D)
    gates = np.stack([a(L0_attn_Wg), a(L0_attn_Wb)]).reshape(2, HG, GH, D)
    w_qkvg = np.concatenate([np.concatenate([*qkv[:, g], *gates[:, g]]) for g in range(HG)]).T
    gate_bias = np.concatenate([a(L0_attn_bg).reshape(HG, GH), a(L0_attn_bb).reshape(HG, GH)], axis=1)
    selector = np.concatenate([np.repeat(np.eye(STEPS), B, axis=1), np.ones((1, P))]).astype(np.float32)
    ins = {
        "patches": patches.reshape(PATCH_TILES, P, KP, P),
        "txt": text,
        "w_patch": blocked(a(L0_tok_W).T),
        "patch_bias": np.concatenate([pos, bias]),
        "w_qkvg": blocked(w_qkvg),
        "gate_bias": np.repeat(gate_bias, B, axis=0),
        "w_out": blocked(a(L0_attn_Wout).T),
        "w_router": blocked(np.concatenate([a(L0_ffn_router_w), a(L0_ffn_shared_gate_w)], axis=1)),
        "w_up": a(L0_ffn_w1).reshape(E, KD, P, F).transpose(2, 0, 1, 3),
        "w_down": a(L0_ffn_w2).reshape(E, KD, P, D).transpose(2, 0, 1, 3),
        "w_shared_up": blocked(L0_ffn_shared_gate_up),
        "w_shared_down": blocked(L0_ffn_shared_down),
        "selector": selector,
        "identity": np.eye(P, dtype=np.float32),
    }
    ins = {k: np.ascontiguousarray(v) for k, v in ins.items()}
    nc = bacc.Bacc("TRN2", target_bir_lowering=False, num_devices=1)
    aps = {k: nc.dram_tensor(k, v.shape, F32, kind="ExternalInput").ap() for k, v in ins.items()}
    out = nc.dram_tensor("out", (TILES, P, D), F32, kind="ExternalOutput").ap()
    fused_block(nc, out=out, **aps)
    got = run_bass_kernel_spmd(nc, [ins], core_ids=[0]).results[0]["out"]
    return got.reshape(T, B, D).transpose(1, 0, 2)
```
